# Optimizing a Trainium2 kernel written in Bass

```python
import numpy as np
import jax
import jax.numpy as jnp

def _softmax(x, axis=-1):
    return jax.nn.softmax(x, axis=axis)

def _gelu(x):
    return jax.nn.gelu(x, approximate=True)

def _silu(x):
    return jax.nn.silu(x)

def _sigmoid(x):
    return jax.nn.sigmoid(x)

def _layernorm(x, axis=-1, eps=1e-05):
    m = jnp.mean(x, axis=axis, keepdims=True)
    v = jnp.var(x, axis=axis, keepdims=True)
    return (x - m) / jnp.sqrt(v + eps)

def _scatter_add(tgt, idx, src, axis=0):
    return tgt.at[idx].add(src)

def _segment_sum(src, seg, n):
    return jax.ops.segment_sum(src, seg, n)
kernel_name = 'mk_conv_preact_d2_conv_nhwc1024_r4_403365'

def setup_inputs(seed: int=0):
    np.random.seed(seed)
    _w = jnp.asarray

    def _rec_inputs():
        import jax
        import jax.numpy as jnp
        _gk = jax.random.key(seed)
        x = -0.000125 + 0.9999 * jax.random.normal(jax.random.fold_in(_gk, 1), (32, 16, 16, 256), jnp.float32)
        return x
    x = _rec_inputs()

    def _L0_conv_setup():
        import math
        import jax, jax.numpy as jnp
        import numpy as np
        WIN = 8
        SHIFT = 4
        HEADS = 16
        LOG100 = math.log(100.0)

        def _rel_position_index(wh, ww):
            ch, cw = np.meshgrid(np.arange(wh), np.arange(ww), indexing='ij')
            coords = np.stack([ch.ravel(), cw.ravel()])
            rel = (coords[:, :, None] - coords[:, None, :]).transpose(1, 2, 0)
            rel[:, :, 0] += wh - 1
            rel[:, :, 1] += ww - 1
            rel[:, :, 0] *= 2 * ww - 1
            return rel.sum(-1).ravel()

        def _coords_table(wh, ww):
            rh = np.arange(-(wh - 1), wh, dtype=np.float32)
            rw = np.arange(-(ww - 1), ww, dtype=np.float32)
            t = np.stack(np.meshgrid(rh, rw, indexing='ij'), axis=-1)[None]
            t[..., 0] /= wh - 1
            t[..., 1] /= ww - 1
            t *= 8.0
            return np.sign(t) * np.log2(np.abs(t) + 1.0) / 3.0

        def _shift_mask(H, W, win, shift):
            m = np.zeros((H, W), np.int32)
            cnt = 0
            for hs in ((0, -win), (-win, -shift), (-shift, None)):
                for ws in ((0, -win), (-win, -shift), (-shift, None)):
                    m[hs[0]:hs[1], ws[0]:ws[1]] = cnt
                    cnt += 1
            nW = H // win * (W // win)
            m = m.reshape(H // win, win, W // win, win).transpose(0, 2, 1, 3).reshape(nW, win * win)
            return m[:, None, :] != m[:, :, None]
        key = jax.random.key(seed)
        ks = jax.random.split(key, 11)
        D, HID = (256, 128)
        s = 0.02
        return {'x': jax.random.normal(ks[0], (32, 16, 16, D), jnp.float32), 'Wq': jax.random.normal(ks[1], (D, D), jnp.float32) * s, 'Wk': jax.random.normal(ks[2], (D, D), jnp.float32) * s, 'Wv': jax.random.normal(ks[3], (D, D), jnp.float32) * s, 'bv': jax.random.normal(ks[4], (D,), jnp.float32) * s, 'Wo': jax.random.normal(ks[5], (D, D), jnp.float32) * s, 'bo': jax.random.normal(ks[6], (D,), jnp.float32) * s, 'logit_scale': jnp.full((HEADS, 1, 1), jnp.log(10.0), jnp.float32), 'cpb_w1': jax.random.normal(ks[7], (HID, 2), jnp.float32) * 0.5, 'cpb_b1': jax.random.normal(ks[8], (HID,), jnp.float32) * 0.1, 'cpb_w2': jax.random.normal(ks[9], (HEADS, HID), jnp.float32) * 0.1}
    _L0_conv_all = _L0_conv_setup()
    _L0_conv_in = {k: v for k, v in _L0_conv_all.items() if k in ('Wq', 'Wk', 'Wv', 'bv', 'Wo', 'bo', 'logit_scale', 'cpb_w1', 'cpb_b1', 'cpb_w2')}
    del _L0_conv_all

    def _L1_conv_setup():
        import math
        import jax, jax.numpy as jnp
        import numpy as np
        WIN = 8
        SHIFT = 4
        HEADS = 16
        LOG100 = math.log(100.0)

        def _rel_position_index(wh, ww):
            ch, cw = np.meshgrid(np.arange(wh), np.arange(ww), indexing='ij')
            coords = np.stack([ch.ravel(), cw.ravel()])
            rel = (coords[:, :, None] - coords[:, None, :]).transpose(1, 2, 0)
            rel[:, :, 0] += wh - 1
            rel[:, :, 1] += ww - 1
            rel[:, :, 0] *= 2 * ww - 1
            return rel.sum(-1).ravel()

        def _coords_table(wh, ww):
            rh = np.arange(-(wh - 1), wh, dtype=np.float32)
            rw = np.arange(-(ww - 1), ww, dtype=np.float32)
            t = np.stack(np.meshgrid(rh, rw, indexing='ij'), axis=-1)[None]
            t[..., 0] /= wh - 1
            t[..., 1] /= ww - 1
            t *= 8.0
            return np.sign(t) * np.log2(np.abs(t) + 1.0) / 3.0

        def _shift_mask(H, W, win, shift):
            m = np.zeros((H, W), np.int32)
            cnt = 0
            for hs in ((0, -win), (-win, -shift), (-shift, None)):
                for ws in ((0, -win), (-win, -shift), (-shift, None)):
                    m[hs[0]:hs[1], ws[0]:ws[1]] = cnt
                    cnt += 1
            nW = H // win * (W // win)
            m = m.reshape(H // win, win, W // win, win).transpose(0, 2, 1, 3).reshape(nW, win * win)
            return m[:, None, :] != m[:, :, None]
        key = jax.random.key(seed)
        ks = jax.random.split(key, 11)
        D, HID = (256, 128)
        s = 0.02
        return {'x': jax.random.normal(ks[0], (32, 16, 16, D), jnp.float32), 'Wq': jax.random.normal(ks[1], (D, D), jnp.float32) * s, 'Wk': jax.random.normal(ks[2], (D, D), jnp.float32) * s, 'Wv': jax.random.normal(ks[3], (D, D), jnp.float32) * s, 'bv': jax.random.normal(ks[4], (D,), jnp.float32) * s, 'Wo': jax.random.normal(ks[5], (D, D), jnp.float32) * s, 'bo': jax.random.normal(ks[6], (D,), jnp.float32) * s, 'logit_scale': jnp.full((HEADS, 1, 1), jnp.log(10.0), jnp.float32), 'cpb_w1': jax.random.normal(ks[7], (HID, 2), jnp.float32) * 0.5, 'cpb_b1': jax.random.normal(ks[8], (HID,), jnp.float32) * 0.1, 'cpb_w2': jax.random.normal(ks[9], (HEADS, HID), jnp.float32) * 0.1}
    _L1_conv_all = _L1_conv_setup()
    _L1_conv_in = {k: v for k, v in _L1_conv_all.items() if k in ('Wq', 'Wk', 'Wv', 'bv', 'Wo', 'bo', 'logit_scale', 'cpb_w1', 'cpb_b1', 'cpb_w2')}
    del _L1_conv_all
    return {'x': x, 'L0_conv_Wq': _L0_conv_in['Wq'], 'L0_conv_Wk': _L0_conv_in['Wk'], 'L0_conv_Wv': _L0_conv_in['Wv'], 'L0_conv_bv': _L0_conv_in['bv'], 'L0_conv_Wo': _L0_conv_in['Wo'], 'L0_conv_bo': _L0_conv_in['bo'], 'L0_conv_logit_scale': _L0_conv_in['logit_scale'], 'L0_conv_cpb_w1': _L0_conv_in['cpb_w1'], 'L0_conv_cpb_b1': _L0_conv_in['cpb_b1'], 'L0_conv_cpb_w2': _L0_conv_in['cpb_w2'], 'L1_conv_Wq': _L1_conv_in['Wq'], 'L1_conv_Wk': _L1_conv_in['Wk'], 'L1_conv_Wv': _L1_conv_in['Wv'], 'L1_conv_bv': _L1_conv_in['bv'], 'L1_conv_Wo': _L1_conv_in['Wo'], 'L1_conv_bo': _L1_conv_in['bo'], 'L1_conv_logit_scale': _L1_conv_in['logit_scale'], 'L1_conv_cpb_w1': _L1_conv_in['cpb_w1'], 'L1_conv_cpb_b1': _L1_conv_in['cpb_b1'], 'L1_conv_cpb_w2': _L1_conv_in['cpb_w2']}

def reference(x, L0_conv_Wq, L0_conv_Wk, L0_conv_Wv, L0_conv_bv, L0_conv_Wo, L0_conv_bo, L0_conv_logit_scale, L0_conv_cpb_w1, L0_conv_cpb_b1, L0_conv_cpb_w2, L1_conv_Wq, L1_conv_Wk, L1_conv_Wv, L1_conv_bv, L1_conv_Wo, L1_conv_bo, L1_conv_logit_scale, L1_conv_cpb_w1, L1_conv_cpb_b1, L1_conv_cpb_w2):
    import jax
    import jax.numpy as jnp

    def _L0_conv_ref(x, Wq, Wk, Wv, bv, Wo, bo, logit_scale, cpb_w1, cpb_b1, cpb_w2):
        import math
        import jax, jax.numpy as jnp
        import numpy as np
        WIN = 8
        SHIFT = 4
        HEADS = 16
        LOG100 = math.log(100.0)

        def _rel_position_index(wh, ww):
            ch, cw = np.meshgrid(np.arange(wh), np.arange(ww), indexing='ij')
            coords = np.stack([ch.ravel(), cw.ravel()])
            rel = (coords[:, :, None] - coords[:, None, :]).transpose(1, 2, 0)
            rel[:, :, 0] += wh - 1
            rel[:, :, 1] += ww - 1
            rel[:, :, 0] *= 2 * ww - 1
            return rel.sum(-1).ravel()

        def _coords_table(wh, ww):
            rh = np.arange(-(wh - 1), wh, dtype=np.float32)
            rw = np.arange(-(ww - 1), ww, dtype=np.float32)
            t = np.stack(np.meshgrid(rh, rw, indexing='ij'), axis=-1)[None]
            t[..., 0] /= wh - 1
            t[..., 1] /= ww - 1
            t *= 8.0
            return np.sign(t) * np.log2(np.abs(t) + 1.0) / 3.0

        def _shift_mask(H, W, win, shift):
            m = np.zeros((H, W), np.int32)
            cnt = 0
            for hs in ((0, -win), (-win, -shift), (-shift, None)):
                for ws in ((0, -win), (-win, -shift), (-shift, None)):
                    m[hs[0]:hs[1], ws[0]:ws[1]] = cnt
                    cnt += 1
            nW = H // win * (W // win)
            m = m.reshape(H // win, win, W // win, win).transpose(0, 2, 1, 3).reshape(nW, win * win)
            return m[:, None, :] != m[:, :, None]
        B, H, W, D = x.shape
        N = WIN * WIN
        d = D // HEADS
        nWh, nWw = (H // WIN, W // WIN)
        nW = nWh * nWw
        xs = jnp.roll(x, (-SHIFT, -SHIFT), axis=(1, 2))
        xw = xs.reshape(B, nWh, WIN, nWw, WIN, D).transpose(0, 1, 3, 2, 4, 5)
        xw = xw.reshape(B * nW, N, D)
        q = (xw @ Wq.T).reshape(-1, N, HEADS, d).transpose(0, 2, 1, 3)
        k = (xw @ Wk.T).reshape(-1, N, HEADS, d).transpose(0, 2, 1, 3)
        v = (xw @ Wv.T + bv).reshape(-1, N, HEADS, d).transpose(0, 2, 1, 3)
        qn = q / jnp.maximum(jnp.linalg.norm(q, axis=-1, keepdims=True), 1e-12)
        kn = k / jnp.maximum(jnp.linalg.norm(k, axis=-1, keepdims=True), 1e-12)
        scale = jnp.exp(jnp.minimum(logit_scale, LOG100))
        logits = jnp.einsum('bhnd,bhmd->bhnm', qn, kn) * scale
        table = jnp.asarray(_coords_table(WIN, WIN))
        hcpb = jax.nn.relu(table @ cpb_w1.T + cpb_b1) @ cpb_w2.T
        tab = hcpb.reshape(-1, HEADS)
        idx = jnp.asarray(_rel_position_index(WIN, WIN))
        bias = tab[idx].reshape(N, N, HEADS).transpose(2, 0, 1)[None]
        logits = logits + 16.0 * jax.nn.sigmoid(bias)
        mask = jnp.asarray(_shift_mask(H, W, WIN, SHIFT))
        lg = logits.reshape(B, nW, HEADS, N, N)
        lg = jnp.where(mask[None, :, None], -jnp.inf, lg)
        logits = lg.reshape(B * nW, HEADS, N, N)
        scores = jax.nn.softmax(logits, axis=-1)
        o = jnp.einsum('bhnm,bhmd->bhnd', scores, v)
        o = o.transpose(0, 2, 1, 3).reshape(B * nW, N, D)
        z = o @ Wo.T + bo
        z = z.reshape(B, nWh, nWw, WIN, WIN, D).transpose(0, 1, 3, 2, 4, 5).reshape(B, H, W, D)
        return jnp.roll(z, (SHIFT, SHIFT), axis=(1, 2))

    def _L1_conv_ref(x, Wq, Wk, Wv, bv, Wo, bo, logit_scale, cpb_w1, cpb_b1, cpb_w2):
        import math
        import jax, jax.numpy as jnp
        import numpy as np
        WIN = 8
        SHIFT = 4
        HEADS = 16
        LOG100 = math.log(100.0)

        def _rel_position_index(wh, ww):
            ch, cw = np.meshgrid(np.arange(wh), np.arange(ww), indexing='ij')
            coords = np.stack([ch.ravel(), cw.ravel()])
            rel = (coords[:, :, None] - coords[:, None, :]).transpose(1, 2, 0)
            rel[:, :, 0] += wh - 1
            rel[:, :, 1] += ww - 1
            rel[:, :, 0] *= 2 * ww - 1
            return rel.sum(-1).ravel()

        def _coords_table(wh, ww):
            rh = np.arange(-(wh - 1), wh, dtype=np.float32)
            rw = np.arange(-(ww - 1), ww, dtype=np.float32)
            t = np.stack(np.meshgrid(rh, rw, indexing='ij'), axis=-1)[None]
            t[..., 0] /= wh - 1
            t[..., 1] /= ww - 1
            t *= 8.0
            return np.sign(t) * np.log2(np.abs(t) + 1.0) / 3.0

        def _shift_mask(H, W, win, shift):
            m = np.zeros((H, W), np.int32)
            cnt = 0
            for hs in ((0, -win), (-win, -shift), (-shift, None)):
                for ws in ((0, -win), (-win, -shift), (-shift, None)):
                    m[hs[0]:hs[1], ws[0]:ws[1]] = cnt
                    cnt += 1
            nW = H // win * (W // win)
            m = m.reshape(H // win, win, W // win, win).transpose(0, 2, 1, 3).reshape(nW, win * win)
            return m[:, None, :] != m[:, :, None]
        B, H, W, D = x.shape
        N = WIN * WIN
        d = D // HEADS
        nWh, nWw = (H // WIN, W // WIN)
        nW = nWh * nWw
        xs = jnp.roll(x, (-SHIFT, -SHIFT), axis=(1, 2))
        xw = xs.reshape(B, nWh, WIN, nWw, WIN, D).transpose(0, 1, 3, 2, 4, 5)
        xw = xw.reshape(B * nW, N, D)
        q = (xw @ Wq.T).reshape(-1, N, HEADS, d).transpose(0, 2, 1, 3)
        k = (xw @ Wk.T).reshape(-1, N, HEADS, d).transpose(0, 2, 1, 3)
        v = (xw @ Wv.T + bv).reshape(-1, N, HEADS, d).transpose(0, 2, 1, 3)
        qn = q / jnp.maximum(jnp.linalg.norm(q, axis=-1, keepdims=True), 1e-12)
        kn = k / jnp.maximum(jnp.linalg.norm(k, axis=-1, keepdims=True), 1e-12)
        scale = jnp.exp(jnp.minimum(logit_scale, LOG100))
        logits = jnp.einsum('bhnd,bhmd->bhnm', qn, kn) * scale
        table = jnp.asarray(_coords_table(WIN, WIN))
        hcpb = jax.nn.relu(table @ cpb_w1.T + cpb_b1) @ cpb_w2.T
        tab = hcpb.reshape(-1, HEADS)
        idx = jnp.asarray(_rel_position_index(WIN, WIN))
        bias = tab[idx].reshape(N, N, HEADS).transpose(2, 0, 1)[None]
        logits = logits + 16.0 * jax.nn.sigmoid(bias)
        mask = jnp.asarray(_shift_mask(H, W, WIN, SHIFT))
        lg = logits.reshape(B, nW, HEADS, N, N)
        lg = jnp.where(mask[None, :, None], -jnp.inf, lg)
        logits = lg.reshape(B * nW, HEADS, N, N)
        scores = jax.nn.softmax(logits, axis=-1)
        o = jnp.einsum('bhnm,bhmd->bhnd', scores, v)
        o = o.transpose(0, 2, 1, 3).reshape(B * nW, N, D)
        z = o @ Wo.T + bo
        z = z.reshape(B, nWh, nWw, WIN, WIN, D).transpose(0, 1, 3, 2, 4, 5).reshape(B, H, W, D)
        return jnp.roll(z, (SHIFT, SHIFT), axis=(1, 2))

    def _gn(v, G=32, eps=1e-05):
        B_, H_, W_, C_ = v.shape
        g = v.reshape(B_, H_, W_, G, C_ // G)
        m = jnp.mean(g, axis=(1, 2, 4), keepdims=True)
        s = jnp.var(g, axis=(1, 2, 4), keepdims=True)
        return ((g - m) / jnp.sqrt(s + eps)).reshape(v.shape)

    def _ln_c(v, eps=1e-06):
        m = jnp.mean(v, axis=-1, keepdims=True)
        s = jnp.var(v, axis=-1, keepdims=True)
        return (v - m) / jnp.sqrt(s + eps)

    def _ln_t(v, eps=1e-05):
        m = jnp.mean(v, axis=-1, keepdims=True)
        s = jnp.var(v, axis=-1, keepdims=True)
        return (v - m) / jnp.sqrt(s + eps)

    def _to_tokens(v):
        B_, H_, W_, C_ = v.shape
        return v.reshape(B_, H_ * W_, C_)

    def _from_tokens(t, like):
        return t.reshape(like.shape)
    x = x + _L0_conv_ref(_gn(x), L0_conv_Wq, L0_conv_Wk, L0_conv_Wv, L0_conv_bv, L0_conv_Wo, L0_conv_bo, L0_conv_logit_scale, L0_conv_cpb_w1, L0_conv_cpb_b1, L0_conv_cpb_w2)
    x = x + _L1_conv_ref(_gn(x), L1_conv_Wq, L1_conv_Wk, L1_conv_Wv, L1_conv_bv, L1_conv_Wo, L1_conv_bo, L1_conv_logit_scale, L1_conv_cpb_w1, L1_conv_cpb_b1, L1_conv_cpb_w2)
    return x

_drawn_inputs = setup_inputs


def setup_inputs(seed=0):
    import zlib

    import numpy as np

    out = dict(_drawn_inputs(seed))
    spreads = {'L0_conv_logit_scale': (2.3025851249694824, 0.6),
     'L1_conv_logit_scale': (2.3025851249694824, 0.6)}
    factors = {'L0_conv_bv': 8.0,
     'L0_conv_bo': 2.696,
     'L0_conv_cpb_b1': 37.632,
     'L1_conv_bv': 8.0,
     'L1_conv_bo': 2.742,
     'L1_conv_cpb_b1': 39.338,
     'L0_conv_cpb_w1': 2.73,
     'L0_conv_cpb_w2': 2.857,
     'L1_conv_cpb_w1': 3.108,
     'L1_conv_cpb_w2': 3.678}
    for name, (base, spread) in spreads.items():
        noise = np.random.default_rng([zlib.crc32(name.encode()), seed]).standard_normal(out[name].shape)
        drawn = base * np.exp(spread * noise) if base else spread * noise
        out[name] = jnp.asarray(drawn.astype(out[name].dtype))
    for name, factor in factors.items():
        out[name] = (out[name] * factor).astype(out[name].dtype)
    return out
```

```python
from contextlib import ExitStack

import concourse.bass as bass
from concourse import mybir

F32 = mybir.dt.float32
F16 = mybir.dt.float16
I32 = mybir.dt.int32
ALU = mybir.AluOpType
ACT = mybir.ActivationFunctionType
AX_X = mybir.AxisListType.X

P = 128
IMAGES, SIDE, D = 32, 16, 256
LAYERS = 2
WIN, SHIFT, HEADS = 8, 4, 16
N = WIN * WIN
HD = D // HEADS
PAIRS = HEADS // 2
CC = D // P
TOKENS = SIDE * SIDE
TILES = TOKENS // P
REL = 2 * WIN - 1
RUN = (WIN - 1) * REL + WIN
AUG = 64
JOBS = LAYERS * IMAGES
BIAS_TOP = 16.0
HEADROOM = 80.0
LOG100 = 4.605170185988092
RSQRT_SEED = 0x5F3759DF
NEWTON = 3
RSQRT_OPS = 1 + 3 * NEWTON


class Job:

    def __init__(self, half, parity, layer):
        self.half, self.parity, self.layer = half, parity, layer

    def __add__(self, k):
        s = self.parity + k
        return Job(self.half + s // 2, s % 2, self.layer)

    def count(self, per_image, done):
        return 2 * per_image * self.half + (per_image * self.parity + done)

    def count_half(self, per_image):
        return per_image * self.half + per_image

    @property
    def image(self):
        return 2 * self.half + (self.parity - IMAGES * self.layer)


def build(nc, x, weights, out, consts, table_scratch):
    with ExitStack() as ctx:
        def sb(name, shape, dt=F32):
            return ctx.enter_context(nc.sbuf_tensor(name, shape, dt))

        def sem(name):
            return ctx.enter_context(nc.semaphore(name))

        L = LAYERS
        ident16 = sb("ident16", [P, P], F16)
        group_mean = sb("group_mean", [P, P])
        coords = sb("coords", [3, REL * REL])
        masks = sb("masks", [P, 4, N])
        w_qk = sb("w_qk", [P, L, CC, 2 * D])
        w_v = sb("w_v", [P, L, CC, D])
        w_o = sb("w_o", [P, L, CC, D])
        bv = sb("bv", [P, L, CC])
        bo = sb("bo", [P, L, CC])
        out_bias = sb("out_bias", [P, L, CC])
        cpb1 = sb("cpb1", [3, L, P])
        cpb2 = sb("cpb2", [P, L, HEADS])
        hidden = sb("hidden", [P, L, REL * REL])
        table = sb("table", [HEADS, L, REL * REL])
        bias_rev = sb("bias_rev", [P, PAIRS, WIN * REL])
        exp_bias = sb("exp_bias", [P, L, 4, PAIRS, N])
        qk_scale = sb("qk_scale", [P, L, 2 * HEADS])
        shift32 = sb("shift32", [P, L, HEADS])
        ones = sb("ones", [P, 32])

        x_all = sb("x_all", [P, IMAGES, CC, TOKENS])
        bn6 = sb("bn6", [P, CC, 2, 3])
        mean_sq = sb("mean_sq", [P, CC, 2])
        g_mom = sb("g_mom", [P, CC, 2])
        g_sq = sb("g_sq", [P, CC])
        g_var = sb("g_var", [P, CC])
        g_tmp = sb("g_tmp", [P, CC])
        g_rstd = sb("g_rstd", [P, CC])
        g_off = sb("g_off", [P, CC])
        xn = sb("xn", [P, 2, CC, TOKENS])
        squares = sb("squares", [P, 2 * D])
        norm2 = sb("norm2", [P, 2 * HEADS])
        n_tmp = sb("n_tmp", [P, 2 * HEADS])
        rnorm = sb("rnorm", [P, 2 * HEADS])
        unit = sb("unit", [P, 2 * D])
        q_aug = sb("q_aug", [P, L, 2, HEADS, AUG], F16)
        k_aug = sb("k_aug", [P, 2, HEADS, AUG], F16)
        q_rows = sb("q_rows", [P, 2, PAIRS, P], F16)
        k_rows = sb("k_rows", [P, 2, 2, PAIRS, P], F16)
        v_pair = sb("v_pair", [P, 4, 2, PAIRS, 32])
        probs = sb("probs", [P, 4, PAIRS, N])
        r_sum = sb("r_sum", [P, CC, P])
        mixed = sb("mixed", [P, 2, CC, TOKENS])
        x_out = sb("x_out", [P, 2, CC, TOKENS])

        ps = [ctx.enter_context(nc.psum_tensor(f"bank{i}", [P, 512], F32)) for i in range(8)]
        b_qk, b_v, b_turn, b_misc = ps[0], ps[1], ps[2], ps[3]
        b_score, b_mix = ps[4:6], ps[6:8]
        turned = b_turn[:, :].bitcast(F16).rearrange("p (g t) -> p g t", g=PAIRS)

        consts_in = sem("consts_in")
        weights_in = sem("weights_in")
        su_pe, su_act, su_dve, su_pool = sem("su_pe"), sem("su_act"), sem("su_dve"), sem("su_pool")
        table_out, bias_in = sem("table_out"), sem("bias_in")
        x_loaded = [sem("x_loaded0"), sem("x_loaded1")]
        bn_step = sem("bn_step")
        aug_zero = sem("aug_zero")
        group_summed = sem("group_summed")
        gn_step = sem("gn_step")
        xn_ready = sem("xn_ready")
        qk_done, v_done = sem("qk_done"), sem("v_done")
        v_ready = sem("v_ready")
        squared = sem("squared")
        rn_step = sem("rn_step")
        unit_ready = sem("unit_ready")
        hi_ready, lo_ready = sem("hi_ready"), sem("lo_ready")
        q_turned, k_turned = sem("q_turned"), sem("k_turned")
        q_ready, k_ready0, k_ready1 = sem("q_ready"), sem("k_ready0"), sem("k_ready1")
        scored, exped, weighted = sem("scored"), sem("exped"), sem("weighted")
        mix_done, sums_inverted, mixed_ready = sem("mix_done"), sem("sums_inverted"), sem("mixed_ready")
        z_done, x_updated = sem("z_done"), sem("x_updated")
        out_stored = [sem("out_stored0"), sem("out_stored1")]

        CONSTS = 5
        PER_LAYER_IN = 4 + 2 * CC + 2 + 1 + 1
        GATHERS = 2 * WIN
        BN_OPS, GN_OPS = CC + 2, 5 + RSQRT_OPS
        SU_ACT_PER_LAYER, SU_DVE_PER_LAYER = 4, 14

        def past(engine, semaphore, value):
            if not (isinstance(value, int) and value <= 0):
                engine.wait_ge(semaphore, value)

        def run(engine, iteration):
            def one(j):
                half, parity = divmod(j, 2)
                iteration(j, Job(half, parity, None))

            def some(layer, a, b):
                for j in range(a, b):
                    one(j)

            some(0, -1, 4)
            for layer in range(LAYERS):
                first = IMAGES * layer + 4
                last = IMAGES * (layer + 1) - 2
                with engine.Fori(first // 2, last // 2) as half:
                    for parity in range(2):
                        iteration(first + parity, Job(half, parity, None))
                some(layer, last, last + (6 if layer + 1 < LAYERS else 4))

        def job(j, base, k):
            if not 0 <= j + k < JOBS:
                return None
            got = base + k
            got.layer = (j + k) // IMAGES
            return got

        block = ctx.enter_context(nc.Block())

        @block.sync
        def _(sp):
            def load_x(t):
                if t is None or t.layer:
                    return
                past(sp, x_loaded[t.parity], 16 * t.half)
                sp.dma_start(x_all[:, bass.ds(t.image, 1), :, :], x[:, bass.ds(t.image, 1), :, :]).then_inc(x_loaded[t.parity], 16)

            def store_x(t):
                if t is None or t.layer == 0:
                    return
                sp.wait_ge(x_updated, t.count(1, 1))
                sp.dma_start(out[:, bass.ds(t.image, 1), :, :], x_out[:, t.parity:t.parity + 1, :, :]).then_inc(out_stored[t.parity], 16)

            load_x(Job(0, 0, 0))
            for dst, name in ((ident16[:, :], "ident16"),
                              (group_mean[:, :], "group_mean"), (coords[:, :], "coords")):
                sp.dma_start(dst, consts[name]).then_inc(consts_in, 16)
            for a in range(2):
                sp.dma_start(masks[N * a:N * a + N, :, :], consts["masks"].rearrange("w m n -> m w n"))\
                  .then_inc(consts_in, 16)
            for l in range(LAYERS):
                w = weights[l]
                for dst, name in ((w_qk[:, l, :, 0:D], "Wq"), (w_qk[:, l, :, D:2 * D], "Wk"), (w_v[:, l, :, :], "Wv"), (w_o[:, l, :, :], "Wo")):
                    sp.dma_start(dst, w[name].rearrange("(c p) o -> p c o", p=P)).then_inc(weights_in, 16)
                for dst, name in ((bv, "bv"), (bo, "bo")):
                    for c in range(CC):
                        sp.dma_start(dst[:, l, c:c + 1], w[name][c * P:(c + 1) * P].rearrange("(p o) -> p o", o=1)).then_inc(weights_in, 16)
                sp.dma_start(cpb1[0:2, l, :], w["cpb_w1"]).then_inc(weights_in, 16)
                sp.dma_start(cpb1[2:3, l, :], w["cpb_b1"].rearrange("(o h) -> o h", o=1)).then_inc(weights_in, 16)
                sp.dma_start(cpb2[:, l, :], w["cpb_w2"]).then_inc(weights_in, 16)
                sp.dma_start(qk_scale[:, l, 0:HEADS],
                             w["logit_scale"].rearrange("(o h) a b -> o (h a b)", o=1).broadcast_to([P, HEADS]))\
                  .then_inc(weights_in, 16)
            for l in range(LAYERS):
                sp.wait_ge(su_act, SU_ACT_PER_LAYER * (l + 1))
                sp.dma_start(table_scratch[l], table[:, l, :]).then_inc(table_out, 16)
                sp.wait_ge(table_out, 16 * (l + 1))
                if l:
                    sp.wait_ge(su_dve, SU_DVE_PER_LAYER * l)
                for a in range(2):
                    for rm in range(WIN):
                        at = table_scratch[l, a, rm * REL:]
                        src = bass.AP(at.tensor, at.offset, [[1, WIN], [2 * REL * REL, PAIRS], [1, RUN]])
                        p0 = N * a + WIN * rm
                        sp.dma_start(bias_rev[p0:p0 + WIN, :, 0:RUN], src)\
                          .then_inc(bias_in, 16)

            def iteration(j, base):
                load_x(job(j, base, 2))
                store_x(job(j, base, -2))

            run(sp, iteration)
            for parity in range(2):
                sp.wait_ge(out_stored[parity], 16 * IMAGES // 2)

        @block.tensor
        def _(pe):
            pe.wait_ge(consts_in, 16 * CONSTS)
            pe.wait_ge(weights_in, 16 * PER_LAYER_IN * LAYERS)
            for l in range(LAYERS):
                for c in range(CC):
                    for k in range(CC):
                        last = nc.tensor.matmul(ps[l][:, c:c + 1], w_o[:, l, k, c * P:(c + 1) * P], bv[:, l, k:k + 1],
                                                start=(k == 0), stop=(k == CC - 1))
                last.then_inc(su_pe, 1)
                nc.tensor.matmul(ps[4 + l][:, 0:REL * REL], cpb1[:, l, :], coords[:, :], start=True, stop=True)\
                    .then_inc(su_pe, 1)
            for l in range(LAYERS):
                pe.wait_ge(su_act, SU_ACT_PER_LAYER * l + 1)
                nc.tensor.matmul(ps[6 + l][0:HEADS, 0:REL * REL], cpb2[:, l, :], hidden[:, l, :], start=True, stop=True)\
                    .then_inc(su_pe, 1)
            pe.wait_ge(su_act, SU_ACT_PER_LAYER * LAYERS)
            pe.wait_ge(su_dve, SU_DVE_PER_LAYER * LAYERS)
            pe.wait_ge(su_pool, 4)

            def sum_groups(j, t):
                if t is None:
                    return
                pe.wait_ge(bn_step, t.count(BN_OPS, BN_OPS))
                past(pe, x_updated, t.count(1, -3))
                for s in range(2):
                    last = nc.tensor.matmul(b_misc[:, 0:2 * CC], group_mean[:, :], bn6[:, :, s, 1:3], start=(s == 0), stop=(s == 1))
                last.then_inc(group_summed, 1)

            def project(t, e):
                if t is None:
                    return
                T1 = t.count(2, e)
                if e == 0:
                    pe.wait_ge(xn_ready, t.count(2, 2))
                past(pe, v_ready, t.count(8, 4 * e))
                for c in range(CC):
                    last = nc.tensor.matmul(b_v[:, 0:D], xn[:, t.parity, c, e * P:(e + 1) * P], w_v[:, t.layer, c, :],
                                            start=(c == 0), stop=(c == CC - 1))
                last.then_inc(v_done, 1)
                past(pe, unit_ready, T1)
                for c in range(CC):
                    last = nc.tensor.matmul(b_qk[:, :], xn[:, t.parity, c, e * P:(e + 1) * P], w_qk[:, t.layer, c, :],
                                            start=(c == 0), stop=(c == CC - 1))
                last.then_inc(qk_done, 1)

            def turn_q(t, e):
                if t is None:
                    return
                T1 = t.count(2, e)
                pe.wait_ge(lo_ready, t.count(4, 2 * e + 2))
                past(pe, k_ready0, T1)
                past(pe, k_ready1, T1)
                for g in range(PAIRS):
                    last = nc.tensor.transpose(turned[:, g, :], q_aug[:, t.layer, e, 2 * g:2 * g + 2, :].rearrange("p a r -> p (a r)"), ident16[:, :])
                last.then_inc(q_turned, 1)

            def turn_k(t, e):
                if t is None:
                    return
                pe.wait_ge(q_ready, t.count(2, e + 1))
                for g in range(PAIRS):
                    last = nc.tensor.transpose(turned[:, g, :], k_aug[:, e, 2 * g:2 * g + 2, :].rearrange("p a r -> p (a r)"), ident16[:, :])
                last.then_inc(k_turned, 1)

            def score(t, e):
                if t is None:
                    return
                T = t.count(2, e + 1)
                pe.wait_ge(q_ready, T)
                pe.wait_ge(k_ready0, T)
                pe.wait_ge(k_ready1, T)
                for w in range(2):
                    past(pe, exped, t.count(4, 2 * e + w - 1))
                    for g in range(PAIRS):
                        last = nc.tensor.matmul(b_score[w][:, g * N:(g + 1) * N], k_rows[:, e, w, g, :],
                                                q_rows[:, e, g, w * N:(w + 1) * N], start=True, stop=True, skip_group_check=True)
                    last.then_inc(scored, 1)

            def mix(t, e):
                if t is None:
                    return
                T1 = t.count(2, e)
                past(pe, mixed_ready, t.count(2, e - 1))
                bank = b_mix[e][:, :].rearrange("p (s c t) -> p s c t", s=2, c=CC)
                pe.wait_ge(v_ready, t.count(8, 4 * e + 4))
                vb = 2 * t.parity + e
                for w in range(2):
                    pe.wait_ge(weighted, t.count(4, 2 * e + w + 1))
                    pr = probs[:, 2 * e + w, :, :]
                    for g in range(PAIRS):
                        c, r = divmod(g, 4)
                        nc.tensor.matmul(bank[32 * r:32 * r + 32, 0, c, w * N:(w + 1) * N], v_pair[:, vb, w, g, :],
                                         pr[:, g, :], start=True, stop=True, skip_group_check=True)
                    for r in range(4):
                        last = nc.tensor.matmul(bank[32 * r:32 * r + 32, 1, :, w * N:(w + 1) * N], ones[:, :],
                                                pr[:, r:PAIRS:4, :], start=True, stop=True, skip_group_check=True)
                last.then_inc(mix_done, 1)

            def project_out(j, t):
                if t is None:
                    return
                pe.wait_ge(mixed_ready, t.count(2, 2))
                if j + 1 < JOBS:
                    pe.wait_ge(gn_step, t.count(GN_OPS, 3 * GN_OPS + 1))
                elif j - 2 > JOBS - 3:
                    pe.wait_ge(x_updated, t.count(1, 0))
                bank = b_misc[:, :].rearrange("p (c t) -> p c t", c=CC)
                for c in range(CC):
                    for k in range(CC):
                        last = nc.tensor.matmul(bank[:, c, :], w_o[:, t.layer, k, c * P:(c + 1) * P], mixed[:, t.parity, k, :],
                                                start=(k == 0), stop=(k == CC - 1), skip_group_check=True)
                last.then_inc(z_done, 1)

            def iteration(j, base):
                now, before, after, two_ago = (job(j, base, k) for k in (0, -1, 1, -2))
                turn_q(before, 1)
                project(now, 0)
                turn_k(before, 1)
                sum_groups(j, after)
                mix(two_ago, 1)
                score(before, 0)
                turn_q(now, 0)
                project(now, 1)
                project_out(j, two_ago)
                turn_k(now, 0)
                mix(before, 0)
                score(before, 1)

            run(pe, iteration)

        @block.scalar
        def _(act):
            for l in range(LAYERS):
                act.wait_ge(su_pe, 2 * l + 2)
                nc.scalar.activation(hidden[:, l, :], ps[4 + l][:, 0:REL * REL], ACT.Relu).then_inc(su_act, 1)
                act.wait_ge(su_dve, SU_DVE_PER_LAYER * l + 1)
                nc.scalar.activation(qk_scale[:, l, 0:HEADS], qk_scale[:, l, 0:HEADS], ACT.Exp).then_inc(su_act, 1)
                act.wait_ge(su_pe, 2 * LAYERS + l + 1)
                nc.scalar.activation(table[:, l, :], ps[6 + l][0:HEADS, 0:REL * REL], ACT.Exp, scale=-1.0).then_inc(su_act, 1)
                act.wait_ge(su_dve, SU_DVE_PER_LAYER * l + 8)
                nc.scalar.activation(table[:, l, :], table[:, l, :], ACT.Exp, scale=BIAS_TOP).then_inc(su_act, 1)

            def keep_q(t, e):
                if t is None:
                    return
                T = t.count(2, e + 1)
                act.wait_ge(q_turned, T)
                past(act, scored, t.count(4, 2 * e - 2))
                nc.scalar.activation(q_rows[:, e, :, :], turned, ACT.Copy).then_inc(q_ready, 1)

            def keep_v(t, e):
                if t is None:
                    return
                T = t.count(2, e + 1)
                act.wait_ge(v_done, T)
                past(act, mix_done, t.count(2, e + 1 - 4))
                v = b_v[:, 0:D].rearrange("p (g a d) -> p g a d", g=PAIRS, a=2)
                for w in range(2):
                    for a in range(2):
                        nc.scalar.activation(v_pair[N * a:N * a + N, 2 * t.parity + e, w, :, HD * a:HD * a + HD],
                                             v[N * w:N * w + N, :, a, :], ACT.Copy).then_inc(v_ready, 1)

            def square(t, e):
                if t is None:
                    return
                T1 = t.count(2, e)
                act.wait_ge(qk_done, t.count(2, e + 1))
                past(act, unit_ready, T1)
                nc.scalar.activation(squares[:, :], b_qk[:, :], ACT.Square).then_inc(squared, 1)

            def keep_k(t, e):
                if t is None:
                    return
                T = t.count(2, e + 1)
                act.wait_ge(k_turned, T)
                past(act, scored, t.count(4, 2 * e - 2))
                nc.scalar.activation(k_rows[0:N, e, :, :, 0:N].rearrange("p w g m -> p g w m"),
                                     turned[0:N, :, :].rearrange("p g (w m) -> p g w m", w=2), ACT.Copy).then_inc(k_ready0, 1)

            def split_hi(t, e):
                if t is None:
                    return
                T = t.count(2, e + 1)
                act.wait_ge(unit_ready, T)
                past(act, k_turned, t.count(2, e - 1))
                for n, dst, step in ((0, q_aug[:, t.layer, e, :, 0:2 * HD], HD), (1, k_aug[:, e, :, 0:4 * HD], 2 * HD)):
                    src = unit[:, n * D:(n + 1) * D].rearrange("p (h o d) -> p h o d", h=HEADS, o=1).broadcast_to([P, HEADS, 2, HD])
                    dst = dst.rearrange("p h (o d) -> p h o d", d=step)[:, :, :, 0:HD]
                    nc.scalar.activation(dst, src, ACT.Copy).then_inc(hi_ready, 1)

            def exp(t, e):
                if t is None:
                    return
                for w in range(2):
                    n = t.count(4, 2 * e + w + 1)
                    act.wait_ge(scored, n)
                    past(act, mix_done, t.count(2, e + 1 - 2))
                    nc.scalar.activation(probs[:, 2 * e + w, :, :].rearrange("p g n -> p (g n)"), b_score[w][:, :], ACT.Exp).then_inc(exped, 1)

            def iteration(j, base):
                now, before, after, two_ago = (job(j, base, k) for k in (0, -1, 1, -2))
                keep_q(before, 1)
                keep_v(now, 0)
                square(now, 0)
                keep_k(before, 1)
                split_hi(now, 0)
                exp(before, 0)
                keep_q(now, 0)
                keep_v(now, 1)
                square(now, 1)
                keep_k(now, 0)
                split_hi(now, 1)
                exp(before, 1)

            run(act, iteration)

        @block.vector
        def _(dve):
            def rsqrt(y, v, tmp, step, count):
                nc.vector.tensor_scalar(y.bitcast(I32), v.bitcast(I32), -0.5, float(RSQRT_SEED), ALU.mult, ALU.add).then_inc(step, 1)
                for k in range(NEWTON):
                    dve.wait_ge(step, count(3 * k + 1))
                    nc.vector.tensor_tensor(tmp, y, y, ALU.mult).then_inc(step, 1)
                    dve.wait_ge(step, count(3 * k + 2))
                    nc.vector.scalar_tensor_tensor(out=tmp, in0=tmp, scalar=-0.5, in1=v, op0=ALU.mult, op1=ALU.mult).then_inc(step, 1)
                    dve.wait_ge(step, count(3 * k + 3))
                    nc.vector.scalar_tensor_tensor(out=y, in0=tmp, scalar=1.5, in1=y, op0=ALU.add, op1=ALU.mult).then_inc(step, 1)

            dve.wait_ge(weights_in, 16 * PER_LAYER_IN * LAYERS)
            dve.wait_ge(consts_in, 16 * CONSTS)
            for l in range(LAYERS):
                b = SU_DVE_PER_LAYER * l
                nc.vector.tensor_scalar(qk_scale[:, l, 0:HEADS], qk_scale[:, l, 0:HEADS], LOG100, None, ALU.min).then_inc(su_dve, 1)
                nc.vector.memset(qk_scale[:, l, HEADS:2 * HEADS], 1.0).then_inc(su_dve, 1)
                dve.wait_ge(su_pe, 2 * l + 1)
                nc.vector.tensor_tensor(out_bias[:, l, :], ps[l][:, 0:CC], bo[:, l, :], ALU.add).then_inc(su_dve, 1)
                dve.wait_ge(su_act, SU_ACT_PER_LAYER * l + 2)
                nc.vector.tensor_scalar(shift32[:, l, :], qk_scale[:, l, 0:HEADS], -1.0, HEADROOM - BIAS_TOP, ALU.mult, ALU.add).then_inc(su_dve, 1)
                dve.wait_ge(su_dve, b + 4)
                dve.wait_ge(su_pool, 2)
                for e in range(2):
                    nc.vector.tensor_copy(q_aug[:, l, e, :, 3 * HD], shift32[:, l, :]).then_inc(su_dve, 1)
                dve.wait_ge(su_act, SU_ACT_PER_LAYER * l + 3)
                nc.vector.tensor_scalar(table[:, l, :], table[:, l, :], 1.0, None, ALU.add).then_inc(su_dve, 1)
                dve.wait_ge(su_dve, b + 7)
                nc.vector.reciprocal(table[:, l, :], table[:, l, :]).then_inc(su_dve, 1)
                for e in range(2):
                    nc.vector.tensor_tensor(q_aug[:, l, e, :, 3 * HD + 1], shift32[:, l, :], q_aug[:, l, e, :, 3 * HD], ALU.subtract).then_inc(su_dve, 1)
                dve.wait_ge(bias_in, 16 * GATHERS * (l + 1))
                rows = bias_rev[:, :, :].rearrange("p g (r c) -> p g r c", c=REL)[:, :, ::-1, WIN - 1::-1]
                for w in range(4):
                    nc.vector.tensor_tensor(exp_bias[:, l, w, :, :].rearrange("p g (r c) -> p g r c", c=WIN), rows,
                                            masks[:, w, :].rearrange("p (o r c) -> p o r c", o=1, c=WIN).broadcast_to([P, PAIRS, WIN, WIN]),
                                            ALU.mult).then_inc(su_dve, 1)
                dve.wait_ge(su_dve, b + SU_DVE_PER_LAYER)

            def group_moments(t):
                if t is None:
                    return
                if t.layer == 0:
                    dve.wait_ge(x_loaded[t.parity], t.count_half(16))
                else:
                    dve.wait_ge(x_updated, t.count(1, 1 - IMAGES))
                past(dve, group_summed, t.count(1, 0))
                for c in range(CC):
                    nc.vector.bn_stats(bn6[:, c, :, :].rearrange("p s m -> p (s m)"),
                                       x_all[:, bass.ds(t.image, 1), c, :].rearrange("p o t -> p (o t)")).then_inc(bn_step, 1)
                dve.wait_ge(bn_step, t.count(BN_OPS, CC))
                nc.vector.tensor_tensor(mean_sq[:, :, :], bn6[:, :, :, 1], bn6[:, :, :, 1], ALU.mult).then_inc(bn_step, 1)
                dve.wait_ge(bn_step, t.count(BN_OPS, CC + 1))
                nc.vector.scalar_tensor_tensor(out=bn6[:, :, :, 2], in0=bn6[:, :, :, 2], scalar=2.0 / TOKENS, in1=mean_sq[:, :, :],
                                               op0=ALU.mult, op1=ALU.add).then_inc(bn_step, 1)

            def group_norm(t):
                if t is None:
                    return
                dve.wait_ge(group_summed, t.count(1, 1))
                s = lambda n: t.count(GN_OPS, n)
                nc.vector.tensor_copy(g_mom[:, :, :].rearrange("p c m -> p (c m)"), b_misc[:, 0:2 * CC]).then_inc(gn_step, 1)
                dve.wait_ge(gn_step, s(1))
                nc.vector.tensor_tensor(g_sq[:, :], g_mom[:, :, 0], g_mom[:, :, 0], ALU.mult).then_inc(gn_step, 1)
                dve.wait_ge(gn_step, s(2))
                nc.vector.tensor_tensor(g_var[:, :], g_mom[:, :, 1], g_sq[:, :], ALU.subtract).then_inc(gn_step, 1)
                dve.wait_ge(gn_step, s(3))
                nc.vector.tensor_scalar(g_var[:, :], g_var[:, :], 0.0, 1e-5, ALU.max, ALU.add).then_inc(gn_step, 1)
                dve.wait_ge(gn_step, s(4))
                rsqrt(g_rstd[:, :], g_var[:, :], g_tmp[:, :], gn_step, lambda n: s(4 + n))
                dve.wait_ge(gn_step, s(4 + RSQRT_OPS))
                nc.vector.scalar_tensor_tensor(out=g_off[:, :], in0=g_mom[:, :, 0], scalar=-1.0, in1=g_rstd[:, :], op0=ALU.mult, op1=ALU.mult).then_inc(gn_step, 1)
                dve.wait_ge(gn_step, s(5 + RSQRT_OPS))
                n = t.count(2, 0)
                past(dve, qk_done, t.count(2, -2))
                for c in range(CC):
                    nc.vector.tensor_scalar(xn[:, t.parity, c, :], x_all[:, bass.ds(t.image, 1), c, :].rearrange("p o t -> p (o t)"),
                                            g_rstd[:, c:c + 1], g_off[:, c:c + 1], ALU.mult, ALU.add).then_inc(xn_ready, 1)

            def make_unit(t, e):
                if t is None:
                    return
                ops = 3 + RSQRT_OPS
                s = lambda n: t.count(2 * ops, ops * e + n)
                dve.wait_ge(squared, t.count(2, e + 1))
                nc.vector.tensor_reduce(norm2[:, :], squares[:, :].rearrange("p (h d) -> p h d", d=HD), AX_X, ALU.add).then_inc(rn_step, 1)
                dve.wait_ge(rn_step, s(1))
                nc.vector.tensor_scalar(norm2[:, :], norm2[:, :], 1e-24, None, ALU.max).then_inc(rn_step, 1)
                dve.wait_ge(rn_step, s(2))
                rsqrt(rnorm[:, :], norm2[:, :], n_tmp[:, :], rn_step, lambda n: s(2 + n))
                dve.wait_ge(rn_step, s(2 + RSQRT_OPS))
                nc.vector.tensor_tensor(rnorm[:, :], rnorm[:, :], qk_scale[:, t.layer, :], ALU.mult).then_inc(rn_step, 1)
                dve.wait_ge(rn_step, s(3 + RSQRT_OPS))
                T1 = t.count(2, e)
                past(dve, lo_ready, t.count(4, 2 * e))
                nc.vector.tensor_tensor(unit[:, :].rearrange("p (h d) -> p h d", d=HD), b_qk[:, :].rearrange("p (h d) -> p h d", d=HD),
                                        rnorm[:, :].rearrange("p (h o) -> p h o", o=1).broadcast_to([P, 2 * HEADS, HD]), ALU.mult).then_inc(unit_ready, 1)

            def keep_k(t, e):
                if t is None:
                    return
                T = t.count(2, e + 1)
                dve.wait_ge(k_turned, T)
                past(dve, scored, t.count(4, 2 * e - 2))
                nc.vector.tensor_copy(k_rows[N:P, e, :, :, N:P].rearrange("p w g m -> p g w m"),
                                      turned[N:P, :, :].rearrange("p g (w m) -> p g w m", w=2)).then_inc(k_ready1, 1)

            def divide(t, e):
                if t is None:
                    return
                T = t.count(2, e + 1)
                dve.wait_ge(mix_done, T)
                bank = b_mix[e][:, :].rearrange("p (s c t) -> p s c t", s=2, c=CC)
                past(dve, mixed_ready, t.count(2, e))
                nc.vector.reciprocal(r_sum[:, :, :], bank[:, 1, :, :]).then_inc(sums_inverted, 1)
                dve.wait_ge(sums_inverted, T)
                past(dve, z_done, t.count(1, -1))
                nc.vector.tensor_tensor(mixed[:, t.parity, :, e * P:(e + 1) * P], bank[:, 0, :, :], r_sum[:, :, :], ALU.mult).then_inc(mixed_ready, 1)

            def add_residual(t):
                if t is None:
                    return
                dve.wait_ge(z_done, t.count(1, 1))
                if t.layer:
                    past(dve, out_stored[t.parity], 16 * t.half - 8 * IMAGES)
                for c in range(CC):
                    here = x_all[:, bass.ds(t.image, 1), c, :].rearrange("p o t -> p (o t)")
                    ins = nc.vector.scalar_tensor_tensor(out=x_out[:, t.parity, c, :] if t.layer else here, in0=b_misc[:, c * TOKENS:(c + 1) * TOKENS],
                                                         scalar=out_bias[:, t.layer, c:c + 1], in1=here, op0=ALU.add, op1=ALU.add)
                ins.then_inc(x_updated, 1)

            def iteration(j, base):
                now, before, after, two_ago = (job(j, base, k) for k in (0, -1, 1, -2))
                group_moments(after)
                keep_k(before, 1)
                make_unit(now, 0)
                group_norm(after)
                divide(two_ago, 1)
                keep_k(now, 0)
                make_unit(now, 1)
                add_residual(two_ago)
                divide(before, 0)

            run(dve, iteration)

        @block.gpsimd
        def _(pool):
            nc.gpsimd.memset(q_aug[:, :, :, :, :], 0.0).then_inc(su_pool, 1)
            nc.gpsimd.memset(ones[:, :], 0.0).then_inc(su_pool, 1)
            nc.gpsimd.memset(k_aug[:, :, :, :], 0.0).then_inc(aug_zero, 1)
            nc.gpsimd.memset(k_rows[:, :, :, :, :], 0.0).then_inc(aug_zero, 1)
            nc.gpsimd.memset(v_pair[:, :, :, :, :], 0.0).then_inc(aug_zero, 1)
            pool.wait_ge(aug_zero, 3)
            pool.wait_ge(su_pool, 2)
            nc.gpsimd.memset(k_aug[:, :, :, 3 * HD:3 * HD + 2], 1.0).then_inc(aug_zero, 1)
            pool.wait_ge(aug_zero, 4)
            nc.gpsimd.memset(ones[0:N, 0:HD], 1.0).then_inc(su_pool, 1)
            nc.gpsimd.memset(ones[N:P, HD:2 * HD], 1.0).then_inc(su_pool, 1)

            def split_lo(t, e):
                if t is None:
                    return
                pool.wait_ge(hi_ready, t.count(4, 2 * e + 2))
                for n, dst, hi in ((0, q_aug[:, t.layer, e, :, 2 * HD:3 * HD], q_aug[:, t.layer, e, :, 0:HD]),
                                   (1, k_aug[:, e, :, HD:2 * HD], k_aug[:, e, :, 0:HD])):
                    nc.gpsimd.tensor_tensor(dst, unit[:, n * D:(n + 1) * D].rearrange("p (h d) -> p h d", d=HD), hi, ALU.subtract).then_inc(lo_ready, 1)

            def weigh(t, e):
                if t is None:
                    return
                for w in range(2):
                    pool.wait_ge(exped, t.count(4, 2 * e + w + 1))
                    pr = probs[:, 2 * e + w, :, :]
                    nc.gpsimd.tensor_tensor(pr, pr, exp_bias[:, t.layer, 2 * e + w, :, :], ALU.mult).then_inc(weighted, 1)

            pool.wait_ge(su_dve, SU_DVE_PER_LAYER * LAYERS)

            def iteration(j, base):
                now, before = (job(j, base, k) for k in (0, -1))
                split_lo(now, 0)
                weigh(before, 0)
                split_lo(now, 1)
                weigh(before, 1)

            run(pool, iteration)


_WEIGHTS = ['Wq', 'Wk', 'Wv', 'bv', 'Wo', 'bo', 'logit_scale', 'cpb_w1', 'cpb_b1', 'cpb_w2']


def _constants():
    import numpy as np
    group = D // 32
    r = np.arange(-(WIN - 1), WIN, dtype=np.float32)
    t = np.stack(np.meshgrid(r, r, indexing="ij"), axis=-1) / (WIN - 1) * 8.0
    t = np.sign(t) * np.log2(np.abs(t) + 1.0) / 3.0
    t = t.reshape(-1, 2)[::-1].T
    pos = np.arange(N)
    low_r, low_c = pos // WIN < WIN - SHIFT, pos % WIN < WIN - SHIFT
    same = [np.ones((N, N), bool), low_c[:, None] == low_c[None, :], low_r[:, None] == low_r[None, :]]
    same.append(same[1] & same[2])
    return {
        "ident16": np.eye(P, dtype=np.float16),
        "group_mean": np.kron(np.eye(P // group), np.full((group, group), 0.5 / group)).astype(np.float32),
        "coords": np.concatenate([t, np.ones((1, REL * REL))]).astype(np.float32),
        "masks": np.stack(same).astype(np.float32),
    }


def _to_channels(x):
    import numpy as np
    x = np.roll(x, (-SHIFT, -SHIFT), axis=(1, 2))
    x = x.reshape(IMAGES, SIDE // WIN, WIN, SIDE // WIN, WIN, CC, P)
    return x.transpose(6, 0, 5, 1, 3, 2, 4).reshape(P, IMAGES, CC, TOKENS)


def _from_channels(y):
    import numpy as np
    y = y.reshape(P, IMAGES, CC, SIDE // WIN, SIDE // WIN, WIN, WIN)
    y = y.transpose(1, 3, 5, 4, 6, 2, 0).reshape(IMAGES, SIDE, SIDE, D)
    return np.roll(y, (SHIFT, SHIFT), axis=(1, 2))


def kernel(**inputs):
    import numpy as _np
    import concourse.bacc as _bacc
    from concourse import mybir as _mybir
    from concourse.bass_utils import run_bass_kernel_spmd as _run

    nc = _bacc.Bacc("TRN2", target_bir_lowering=False, num_devices=1)
    arrays = {}

    def put(name, a):
        a = _np.ascontiguousarray(a)
        arrays[name] = a
        return nc.dram_tensor(name, a.shape, _mybir.dt.from_np(a.dtype), kind="ExternalInput").ap()

    x = put("in_x", _to_channels(_np.asarray(inputs["x"])))
    weights = []
    for l in range(LAYERS):
        w = {n: _np.asarray(inputs[f"L{l}_conv_{n}"]) for n in _WEIGHTS}
        weights.append({n: put(f"in_L{l}_{n}", a.T if a.ndim == 2 else a) for n, a in w.items()})
    consts = {name: put(f"const_{name}", a) for name, a in _constants().items()}
    scratch = nc.dram_tensor("table_scratch", (LAYERS, HEADS, REL * REL), F32, kind="Internal").ap()
    out = nc.dram_tensor("out_0", (P, IMAGES, CC, TOKENS), F32, kind="ExternalOutput").ap()
    build(nc, x, weights, out, consts, scratch)
    r = _run(nc, [arrays], core_ids=[0])
    return _from_channels(r.results[0]["out_0"])
```

```python
import math
from contextlib import ExitStack

import concourse.bass as bass
from concourse import mybir

F32 = mybir.dt.float32
F16 = mybir.dt.float16
I32 = mybir.dt.int32
ALU = mybir.AluOpType
ACT = mybir.ActivationFunctionType
AX_X = mybir.AxisListType.X

P = 128
IMAGES, SIDE, D = 32, 16, 256
LAYERS = 2
WIN, SHIFT, HEADS = 8, 4, 16
N = WIN * WIN
HD = D // HEADS
PAIRS = HEADS // 2
CC = D // P
TOKENS = SIDE * SIDE
TILES = TOKENS // P
REL = 2 * WIN - 1
STEPS_BACK = 3
RUN = (WIN - 1) * REL + WIN
AUG = 64
NORMS = 2 * HEADS
JOBS = LAYERS * IMAGES
BIAS_TOP = 16.0
BIAS_MID = BIAS_TOP / 2
HEADROOM = 75.0
LOG100 = 4.605170185988092
EPS_GN = 1e-5
INV_NORM_TOP = 1e12
LN_SCALE = 2.0 ** 32
LN_FLOOR = 1e-28


class Job:

    def __init__(self, half, parity, layer):
        self.half, self.parity, self.layer = half, parity, layer

    def __add__(self, k):
        s = self.parity + k
        return Job(self.half + s // 2, s % 2, self.layer)

    def count(self, per_image, done):
        return 2 * per_image * self.half + (per_image * self.parity + done)

    def count_half(self, per_image):
        return per_image * self.half + per_image

    @property
    def image(self):
        return 2 * self.half + (self.parity - IMAGES * self.layer)


def build(nc, x, weights, out, consts, table_scratch):
    with ExitStack() as ctx:
        def sb(name, shape, dt=F32):
            return ctx.enter_context(nc.sbuf_tensor(name, shape, dt))

        def sem(name):
            return ctx.enter_context(nc.semaphore(name))

        L = LAYERS
        ident16 = sb("ident16", [P, P], F16)
        group_mean = sb("group_mean", [P, P])
        coords = sb("coords", [3, REL * REL])
        masks = sb("masks", [P, 4, N])
        w_qk = sb("w_qk", [P, L, CC, 2 * D])
        w_v = sb("w_v", [P, L, CC, D])
        w_o = sb("w_o", [P, L, CC, D])
        bv = sb("bv", [P, L, CC])
        bo = sb("bo", [P, L, CC])
        out_bias = sb("out_bias", [P, L, CC])
        cpb1 = sb("cpb1", [3, L, P])
        cpb2 = sb("cpb2", [P, L, HEADS])
        hidden = sb("hidden", [P, L, REL * REL])
        table = sb("table", [HEADS, L, REL * REL])
        bias_rev = sb("bias_rev", [P, PAIRS, WIN * REL])
        exp_bias = sb("exp_bias", [P, L, 4, PAIRS, N])
        qk_scale = sb("qk_scale", [P, L, 2 * HEADS])
        shift32 = sb("shift32", [P, L, HEADS])
        sum_cols = sb("sum_cols", [P, 4, 32])
        act_bias = sb("act_bias", [P, 3])

        x_all = sb("x_all", [P, IMAGES, CC, TOKENS])
        bn6 = sb("bn6", [P, CC, 2, 3])
        mean_sq = sb("mean_sq", [P, CC, 2])
        g_mom = sb("g_mom", [P, CC, 2])
        g_sq = sb("g_sq", [P, CC])
        g_off = sb("g_off", [P, CC])
        xn = sb("xn", [P, 2, CC, TOKENS])
        squares = sb("squares", [P, 2 * D])
        sums = sb("sums", [P, NORMS + CC])
        logs = sb("logs", [P, NORMS + CC])
        newton = sb("newton", [P, NORMS + CC])
        inv_root = sb("inv_root", [P, NORMS + CC])
        rnorm = sb("rnorm", [P, NORMS])
        unit = sb("unit", [P, 2 * D])
        q_aug = sb("q_aug", [P, L, 2, HEADS, AUG], F16)
        k_aug = sb("k_aug", [P, 2, HEADS, AUG], F16)
        q_rows = sb("q_rows", [P, 2, PAIRS, P], F16)
        k_rows = sb("k_rows", [P, 2, 2, PAIRS, P], F16)
        v_pair = sb("v_pair", [P, 4, 2, PAIRS, 32])
        probs = sb("probs", [P, 4, PAIRS, N])
        inv_sums = sb("inv_sums", [P, N])
        top_inverse = sb("top_inverse", [P, N])
        r_sum = sb("r_sum", [P, CC, P])
        mixed = sb("mixed", [P, 2, CC, P])
        x_out = sb("x_out", [P, 2, CC, TOKENS])

        ps = [ctx.enter_context(nc.psum_tensor(f"bank{i}", [P, 512], F32)) for i in range(8)]
        b_qk, b_turn, b_score, b_mix = ps[0:2], ps[2], ps[4:6], ps[6:8]
        v_cols = ps[3][:, 0:D]
        z_cols = ps[3][:, 0:CC * P].rearrange("p (c t) -> p c t", c=CC)
        g_cols = ps[3][:, 0:2 * CC]
        mix_cols = [b[:, 0:CC * P].rearrange("p (c t) -> p c t", c=CC) for b in b_mix]
        sum_rows = [b[:, CC * P:CC * P + N] for b in b_mix]
        turned = b_turn[:, :].bitcast(F16).rearrange("p (g t) -> p g t", g=PAIRS)

        consts_in = sem("consts_in")
        weights_in = sem("weights_in")
        su_pe, su_act, su_dve, su_pool = sem("su_pe"), sem("su_act"), sem("su_dve"), sem("su_pool")
        table_out, bias_in = sem("table_out"), sem("bias_in")
        x_loaded = [sem("x_loaded0"), sem("x_loaded1")]
        bn_step = sem("bn_step")
        aug_zero = sem("aug_zero")
        group_summed = sem("group_summed")
        gn_step = sem("gn_step")
        logged, seeded, newton_step = sem("logged"), sem("seeded"), sem("newton_step")
        xn_ready = sem("xn_ready")
        qk_done, v_done = sem("qk_done"), sem("v_done")
        v_ready = sem("v_ready")
        squared = sem("squared")
        norms_summed, rnorm_ready = sem("norms_summed"), sem("rnorm_ready")
        unit_ready = sem("unit_ready")
        hi_ready, lo_ready = sem("hi_ready"), sem("lo_ready")
        q_turned, k_turned = sem("q_turned"), sem("k_turned")
        q_ready, k_ready0, k_ready1 = sem("q_ready"), sem("k_ready0"), sem("k_ready1")
        scored, exped, weighted = sem("scored"), sem("exped"), sem("weighted")
        mix_done, sums_inverted, sums_spread, mixed_ready = sem("mix_done"), sem("sums_inverted"), sem("sums_spread"), sem("mixed_ready")
        sums_seen = sem("sums_seen")
        z_done, x_updated = sem("z_done"), sem("x_updated")
        out_stored = [sem("out_stored0"), sem("out_stored1")]

        CONSTS = 7
        PER_LAYER_IN = 4 + 2 * CC + 2 + 1 + 1
        GATHERS = 2 * WIN
        BN_OPS, GN_OPS = CC + 2, 5
        SU_ACT_PER_LAYER, SU_DVE_PER_LAYER = 4, 14
        SU_POOL = 2

        def past(engine, semaphore, value):
            if not (isinstance(value, int) and value <= 0):
                engine.wait_ge(semaphore, value)

        def run(engine, iteration):
            def one(j):
                half, parity = divmod(j, 2)
                iteration(j, Job(half, parity, None))

            def some(layer, a, b):
                for j in range(a, b):
                    one(j)

            some(0, -1, 6)
            for layer in range(LAYERS):
                first = IMAGES * layer + 6
                last = IMAGES * (layer + 1) - 2
                with engine.Fori(first // 2, last // 2) as half:
                    for parity in range(2):
                        iteration(first + parity, Job(half, parity, None))
                some(layer, last, last + (8 if layer + 1 < LAYERS else 2 + STEPS_BACK))

        def tile(j, base, e, back):
            k = (e - back) // 2
            return job(j, base, k), e - back - 2 * k

        def job(j, base, k):
            if not 0 <= j + k < JOBS:
                return None
            got = base + k
            got.layer = (j + k) // IMAGES
            return got

        def root_columns(t, after):
            if t is None and after is None:
                return None
            return slice(0 if t is not None else NORMS, NORMS + CC if after is not None else NORMS)

        block = ctx.enter_context(nc.Block())

        @block.sync
        def _(sp):
            def load_x(t):
                if t is None or t.layer:
                    return
                past(sp, x_loaded[t.parity], 16 * t.half)
                sp.dma_start(x_all[:, bass.ds(t.image, 1), :, :], x[:, bass.ds(t.image, 1), :, :]).then_inc(x_loaded[t.parity], 16)

            def store_x(t):
                if t is None or t.layer == 0:
                    return
                sp.wait_ge(x_updated, t.count(2, 2))
                sp.dma_start(out[:, bass.ds(t.image, 1), :, :], x_out[:, t.parity:t.parity + 1, :, :]).then_inc(out_stored[t.parity], 16)

            load_x(Job(0, 0, 0))
            for dst, name in ((ident16[:, :], "ident16"),
                              (group_mean[:, :], "group_mean"), (coords[:, :], "coords"),
                              (sum_cols[:, :, :], "sum_cols"), (act_bias[:, :], "act_bias")):
                sp.dma_start(dst, consts[name]).then_inc(consts_in, 16)
            for a in range(2):
                sp.dma_start(masks[N * a:N * a + N, :, :], consts["masks"].rearrange("w m n -> m w n"))\
                  .then_inc(consts_in, 16)
            for l in range(LAYERS):
                w = weights[l]
                for dst, name in ((w_qk[:, l, :, 0:D], "Wq"), (w_qk[:, l, :, D:2 * D], "Wk"), (w_v[:, l, :, :], "Wv"), (w_o[:, l, :, :], "Wo")):
                    sp.dma_start(dst, w[name].rearrange("(c p) o -> p c o", p=P)).then_inc(weights_in, 16)
                for dst, name in ((bv, "bv"), (bo, "bo")):
                    for c in range(CC):
                        sp.dma_start(dst[:, l, c:c + 1], w[name][c * P:(c + 1) * P].rearrange("(p o) -> p o", o=1)).then_inc(weights_in, 16)
                sp.dma_start(cpb1[0:2, l, :], w["cpb_w1"]).then_inc(weights_in, 16)
                sp.dma_start(cpb1[2:3, l, :], w["cpb_b1"].rearrange("(o h) -> o h", o=1)).then_inc(weights_in, 16)
                sp.dma_start(cpb2[:, l, :], w["cpb_w2"]).then_inc(weights_in, 16)
                sp.dma_start(qk_scale[:, l, 0:HEADS],
                             w["logit_scale"].rearrange("(o h) a b -> o (h a b)", o=1).broadcast_to([P, HEADS]))\
                  .then_inc(weights_in, 16)
            for l in range(LAYERS):
                sp.wait_ge(su_act, SU_ACT_PER_LAYER * (l + 1))
                sp.dma_start(table_scratch[l], table[:, l, :]).then_inc(table_out, 16)
                sp.wait_ge(table_out, 16 * (l + 1))
                if l:
                    sp.wait_ge(su_dve, SU_DVE_PER_LAYER * l)
                for a in range(2):
                    for rm in range(WIN):
                        at = table_scratch[l, a, rm * REL:]
                        src = bass.AP(at.tensor, at.offset, [[1, WIN], [2 * REL * REL, PAIRS], [1, RUN]])
                        p0 = N * a + WIN * rm
                        sp.dma_start(bias_rev[p0:p0 + WIN, :, 0:RUN], src)\
                          .then_inc(bias_in, 16)

            def iteration(j, base):
                load_x(job(j, base, 2))
                store_x(job(j, base, -3))

            run(sp, iteration)
            for parity in range(2):
                sp.wait_ge(out_stored[parity], 16 * IMAGES // 2)

        @block.tensor
        def _(pe):
            pe.wait_ge(consts_in, 16 * CONSTS)
            pe.wait_ge(weights_in, 16 * PER_LAYER_IN * LAYERS)
            for l in range(LAYERS):
                for c in range(CC):
                    for k in range(CC):
                        last = nc.tensor.matmul(ps[l][:, c:c + 1], w_o[:, l, k, c * P:(c + 1) * P], bv[:, l, k:k + 1],
                                                start=(k == 0), stop=(k == CC - 1))
                last.then_inc(su_pe, 1)
                nc.tensor.matmul(ps[4 + l][:, 0:REL * REL], cpb1[:, l, :], coords[:, :], start=True, stop=True)\
                    .then_inc(su_pe, 1)
            for l in range(LAYERS):
                pe.wait_ge(su_act, SU_ACT_PER_LAYER * l + 1)
                nc.tensor.matmul(ps[6 + l][0:HEADS, 0:REL * REL], cpb2[:, l, :], hidden[:, l, :], start=True, stop=True)\
                    .then_inc(su_pe, 1)
            pe.wait_ge(su_act, SU_ACT_PER_LAYER * LAYERS)
            pe.wait_ge(su_dve, SU_DVE_PER_LAYER * LAYERS)
            pe.wait_ge(su_pool, SU_POOL)
            pe.wait_ge(aug_zero, 4)

            def sum_groups(t):
                if t is None:
                    return
                past(pe, v_ready, t.count(8, -4))
                pe.wait_ge(bn_step, t.count(BN_OPS, BN_OPS))
                for s in range(2):
                    last = nc.tensor.matmul(g_cols, group_mean[:, :], bn6[:, :, s, 1:3], start=(s == 0), stop=(s == 1), skip_group_check=True)
                last.then_inc(group_summed, 1)

            def project_qk(t, e):
                if t is None:
                    return
                if e == 0:
                    pe.wait_ge(xn_ready, t.count(2, 2))
                past(pe, unit_ready, t.count(2, e - 1))
                for c in range(CC):
                    last = nc.tensor.matmul(b_qk[e][:, :], xn[:, t.parity, c, e * P:(e + 1) * P], w_qk[:, t.layer, c, :],
                                            start=(c == 0), stop=(c == CC - 1))
                last.then_inc(qk_done, 1)

            def project_v(t, e, after):
                if t is None:
                    return
                if after is not None:
                    pe.wait_ge(gn_step, after.count(GN_OPS, 1))
                past(pe, v_ready, t.count(8, 4 * e))
                past(pe, x_updated, t.count(2, e - 4))
                for c in range(CC):
                    last = nc.tensor.matmul(v_cols, xn[:, t.parity, c, e * P:(e + 1) * P], w_v[:, t.layer, c, :],
                                            start=(c == 0), stop=(c == CC - 1), skip_group_check=True)
                last.then_inc(v_done, 1)

            def turn_q(t, e):
                if t is None:
                    return
                T1 = t.count(2, e)
                pe.wait_ge(hi_ready, t.count(4, 2 * e + 2))
                pe.wait_ge(lo_ready, t.count(4, 2 * e + 2))
                past(pe, k_ready0, T1)
                past(pe, k_ready1, T1)
                for g in range(PAIRS):
                    last = nc.tensor.transpose(turned[:, g, :], q_aug[:, t.layer, e, 2 * g:2 * g + 2, :].rearrange("p a r -> p (a r)"), ident16[:, :])
                last.then_inc(q_turned, 1)

            def turn_k(t, e):
                if t is None:
                    return
                pe.wait_ge(q_ready, t.count(2, e + 1))
                for g in range(PAIRS):
                    last = nc.tensor.transpose(turned[:, g, :], k_aug[:, e, 2 * g:2 * g + 2, :].rearrange("p a r -> p (a r)"), ident16[:, :])
                last.then_inc(k_turned, 1)

            def score(t, e):
                if t is None:
                    return
                T = t.count(2, e + 1)
                pe.wait_ge(q_ready, T)
                pe.wait_ge(k_ready0, T)
                pe.wait_ge(k_ready1, T)
                for w in range(2):
                    past(pe, exped, t.count(4, 2 * e + w - 1))
                    for g in range(PAIRS):
                        last = nc.tensor.matmul(b_score[w][:, g * N:(g + 1) * N], k_rows[:, e, w, g, :],
                                                q_rows[:, e, g, w * N:(w + 1) * N], start=True, stop=True, skip_group_check=True)
                    last.then_inc(scored, 1)

            def mix(t, e):
                if t is None:
                    return
                past(pe, mixed_ready, t.count(2, e - 1))
                pe.wait_ge(v_ready, t.count(8, 4 * e + 4))
                vb = 2 * t.parity + e
                for w in range(2):
                    pe.wait_ge(weighted, t.count(4, 2 * e + w + 1))
                    for g in range(PAIRS):
                        c, r = divmod(g, 4)
                        nc.tensor.matmul(mix_cols[e][32 * r:32 * r + 32, c, w * N:(w + 1) * N], v_pair[:, vb, w, g, :],
                                         probs[:, 2 * e + w, g, :], start=True, stop=True, skip_group_check=True)
                for w in range(2):
                    for c in range(CC):
                        for r in range(4):
                            last = nc.tensor.matmul(sum_rows[e][32 * r:32 * r + 32, :], sum_cols[:, 2 * w + c, :], probs[:, 2 * e + w, 4 * c + r, :],
                                                    start=(w == 0 and c == 0), stop=(w == 1 and c == CC - 1), skip_group_check=True)
                last.then_inc(mix_done, 1)

            def project_out(t, e, after, newest, newest_e):
                if t is None:
                    return
                pe.wait_ge(mixed_ready, t.count(2, e + 1))
                if after is not None:
                    pe.wait_ge(gn_step, after.count(GN_OPS, 1))
                if newest is not None:
                    pe.wait_ge(v_ready, newest.count(8, 4 * newest_e + 4))
                else:
                    pe.wait_ge(x_updated, t.count(2, e))
                for c in range(CC):
                    for k in range(CC):
                        last = nc.tensor.matmul(z_cols[:, c, :], w_o[:, t.layer, k, c * P:(c + 1) * P], mixed[:, e, k, :],
                                                start=(k == 0), stop=(k == CC - 1), skip_group_check=True)
                last.then_inc(z_done, 1)

            def iteration(j, base):
                for e in range(2):
                    after = job(j, base, 1) if e else None
                    turn_q(*tile(j, base, e, 2))
                    sum_groups(after)
                    project_qk(*tile(j, base, e, 0))
                    project_out(*tile(j, base, e, 5), after, *tile(j, base, e, 1))
                    turn_k(*tile(j, base, e, 2))
                    mix(*tile(j, base, e, 4))
                    score(*tile(j, base, e, 3))
                    project_v(*tile(j, base, e, 0), after)

            run(pe, iteration)

        @block.scalar
        def _(act):
            nc.scalar.preload_act_table_set("natural_log_exp_and_others")
            act.wait_ge(consts_in, 16 * CONSTS)
            for l in range(LAYERS):
                act.wait_ge(su_pe, 2 * l + 2)
                nc.scalar.activation(hidden[:, l, :], ps[4 + l][:, 0:REL * REL], ACT.Relu).then_inc(su_act, 1)
                act.wait_ge(su_dve, SU_DVE_PER_LAYER * l + 1)
                nc.scalar.activation(qk_scale[:, l, 0:HEADS], qk_scale[:, l, 0:HEADS], ACT.Exp).then_inc(su_act, 1)
                act.wait_ge(su_pe, 2 * LAYERS + l + 1)
                nc.scalar.activation(table[:, l, :], ps[6 + l][0:HEADS, 0:REL * REL], ACT.Exp, scale=-1.0).then_inc(su_act, 1)
                act.wait_ge(su_dve, SU_DVE_PER_LAYER * l + 8)
                nc.scalar.activation(table[:, l, :], table[:, l, :], ACT.Exp, bias=act_bias[0:HEADS, 0:1], scale=BIAS_TOP).then_inc(su_act, 1)

            def keep_q(t, e):
                if t is None:
                    return
                T = t.count(2, e + 1)
                act.wait_ge(q_turned, T)
                past(act, scored, t.count(4, 2 * e - 2))
                nc.scalar.activation(q_rows[:, e, :, :], turned, ACT.Copy).then_inc(q_ready, 1)

            def keep_v(t, e):
                if t is None:
                    return
                T = t.count(2, e + 1)
                act.wait_ge(v_done, T)
                past(act, mix_done, t.count(2, e + 1 - 4))
                v = v_cols.rearrange("p (g a d) -> p g a d", g=PAIRS, a=2)
                for w in range(2):
                    for a in range(2):
                        nc.scalar.activation(v_pair[N * a:N * a + N, 2 * t.parity + e, w, :, HD * a:HD * a + HD],
                                             v[N * w:N * w + N, :, a, :], ACT.Copy).then_inc(v_ready, 1)

            def square(t, e):
                if t is None:
                    return
                act.wait_ge(qk_done, t.count(2, e + 1))
                past(act, norms_summed, t.count(2, e))
                nc.scalar.activation(squares[:, :], b_qk[e][:, :], ACT.Square).then_inc(squared, 1)

            def seed_roots(j, base, e):
                t, after = job(j, base, 0), job(j, base, 1) if e else None
                at = root_columns(t, after)
                if at is None:
                    return
                if t is not None:
                    act.wait_ge(norms_summed, t.count(2, e + 1))
                if after is not None:
                    act.wait_ge(gn_step, after.count(GN_OPS, 4))
                chain = base.count(2, e + 1)
                past(act, seeded, chain)
                nc.scalar.activation(logs[:, at], sums[:, at], ACT.Ln, bias=act_bias[:, 1:2], scale=LN_SCALE).then_inc(logged, 1)
                act.wait_ge(logged, base.count(2, e + 2))
                past(act, rnorm_ready, t.count(2, e) if t is not None else 0)
                past(act, xn_ready, base.count(2, 2) if after is not None else 0)
                nc.scalar.activation(inv_root[:, at], logs[:, at], ACT.Exp, bias=act_bias[:, 2:3], scale=-0.5).then_inc(seeded, 1)

            def keep_k(t, e):
                if t is None:
                    return
                T = t.count(2, e + 1)
                act.wait_ge(k_turned, T)
                past(act, scored, t.count(4, 2 * e - 2))
                nc.scalar.activation(k_rows[0:N, e, :, :, 0:N].rearrange("p w g m -> p g w m"),
                                     turned[0:N, :, :].rearrange("p g (w m) -> p g w m", w=2), ACT.Copy).then_inc(k_ready0, 1)

            def split_hi(t, e):
                if t is None:
                    return
                T = t.count(2, e + 1)
                act.wait_ge(unit_ready, T)
                past(act, k_turned, t.count(2, e - 1))
                for n, dst, step in ((0, q_aug[:, t.layer, e, :, 0:2 * HD], HD), (1, k_aug[:, e, :, 0:4 * HD], 2 * HD)):
                    src = unit[:, n * D:(n + 1) * D].rearrange("p (h o d) -> p h o d", h=HEADS, o=1).broadcast_to([P, HEADS, 2, HD])
                    dst = dst.rearrange("p h (o d) -> p h o d", d=step)[:, :, :, 0:HD]
                    nc.scalar.activation(dst, src, ACT.Copy).then_inc(hi_ready, 1)

            def exp(t, e, w):
                if t is None:
                    return
                act.wait_ge(scored, t.count(4, 2 * e + w + 1))
                past(act, mix_done, t.count(2, e + 1 - 2))
                nc.scalar.activation(probs[:, 2 * e + w, :, :].rearrange("p g n -> p (g n)"), b_score[w][:, :], ACT.Exp).then_inc(exped, 1)

            def iteration(j, base):
                for e in range(2):
                    keep_v(*tile(j, base, e, 1))
                    keep_q(*tile(j, base, e, 2))
                    split_hi(*tile(j, base, e, 1))
                    square(*tile(j, base, e, 0))
                    seed_roots(j, base, e)
                    keep_k(*tile(j, base, e, 2))
                    exp(*tile(j, base, e, 3), 0)
                    exp(*tile(j, base, e, 3), 1)

            run(act, iteration)

        @block.vector
        def _(dve):
            dve.wait_ge(weights_in, 16 * PER_LAYER_IN * LAYERS)
            dve.wait_ge(consts_in, 16 * CONSTS)
            for l in range(LAYERS):
                b = SU_DVE_PER_LAYER * l
                nc.vector.tensor_scalar(qk_scale[:, l, 0:HEADS], qk_scale[:, l, 0:HEADS], LOG100, None, ALU.min).then_inc(su_dve, 1)
                nc.vector.memset(qk_scale[:, l, HEADS:2 * HEADS], 1.0).then_inc(su_dve, 1)
                dve.wait_ge(su_pe, 2 * l + 1)
                nc.vector.tensor_tensor(out_bias[:, l, :], ps[l][:, 0:CC], bo[:, l, :], ALU.add).then_inc(su_dve, 1)
                dve.wait_ge(su_act, SU_ACT_PER_LAYER * l + 2)
                nc.vector.tensor_scalar(shift32[:, l, :], qk_scale[:, l, 0:HEADS], -1.0, HEADROOM, ALU.mult, ALU.add).then_inc(su_dve, 1)
                dve.wait_ge(su_dve, b + 4)
                dve.wait_ge(su_pool, 1)
                for e in range(2):
                    nc.vector.tensor_copy(q_aug[:, l, e, :, 3 * HD], shift32[:, l, :]).then_inc(su_dve, 1)
                dve.wait_ge(su_act, SU_ACT_PER_LAYER * l + 3)
                nc.vector.tensor_scalar(table[:, l, :], table[:, l, :], 1.0, None, ALU.add).then_inc(su_dve, 1)
                dve.wait_ge(su_dve, b + 7)
                nc.vector.reciprocal(table[:, l, :], table[:, l, :]).then_inc(su_dve, 1)
                for e in range(2):
                    nc.vector.tensor_tensor(q_aug[:, l, e, :, 3 * HD + 1], shift32[:, l, :], q_aug[:, l, e, :, 3 * HD], ALU.subtract).then_inc(su_dve, 1)
                dve.wait_ge(bias_in, 16 * GATHERS * (l + 1))
                rows = bias_rev[:, :, :].rearrange("p g (r c) -> p g r c", c=REL)[:, :, ::-1, WIN - 1::-1]
                for w in range(4):
                    nc.vector.tensor_tensor(exp_bias[:, l, w, :, :].rearrange("p g (r c) -> p g r c", c=WIN), rows,
                                            masks[:, w, :].rearrange("p (o r c) -> p o r c", o=1, c=WIN).broadcast_to([P, PAIRS, WIN, WIN]),
                                            ALU.mult).then_inc(su_dve, 1)
                dve.wait_ge(su_dve, b + SU_DVE_PER_LAYER)

            def group_moments(t):
                if t is None:
                    return
                if t.layer == 0:
                    dve.wait_ge(x_loaded[t.parity], t.count_half(16))
                else:
                    dve.wait_ge(x_updated, t.count(2, 2 - 2 * IMAGES))
                past(dve, group_summed, t.count(1, 0))
                for c in range(CC):
                    nc.vector.bn_stats(bn6[:, c, :, :].rearrange("p s m -> p (s m)"),
                                       x_all[:, bass.ds(t.image, 1), c, :].rearrange("p o t -> p (o t)")).then_inc(bn_step, 1)
                dve.wait_ge(bn_step, t.count(BN_OPS, CC))
                nc.vector.tensor_tensor(mean_sq[:, :, :], bn6[:, :, :, 1], bn6[:, :, :, 1], ALU.mult).then_inc(bn_step, 1)
                dve.wait_ge(bn_step, t.count(BN_OPS, CC + 1))
                nc.vector.scalar_tensor_tensor(out=bn6[:, :, :, 2], in0=bn6[:, :, :, 2], scalar=2.0 / TOKENS, in1=mean_sq[:, :, :],
                                               op0=ALU.mult, op1=ALU.add).then_inc(bn_step, 1)

            def group_variance(t, n):
                if t is None:
                    return
                if n == 0:
                    dve.wait_ge(group_summed, t.count(1, 1))
                    nc.vector.tensor_copy(g_mom[:, :, :].rearrange("p c m -> p (c m)"), g_cols).then_inc(gn_step, 1)
                else:
                    dve.wait_ge(gn_step, t.count(GN_OPS, n))
                if n == 1:
                    nc.vector.tensor_tensor(g_sq[:, :], g_mom[:, :, 0], g_mom[:, :, 0], ALU.mult).then_inc(gn_step, 1)
                if n == 2:
                    nc.vector.tensor_tensor(g_sq[:, :], g_mom[:, :, 1], g_sq[:, :], ALU.subtract).then_inc(gn_step, 1)
                if n == 3:
                    nc.vector.tensor_scalar(sums[:, NORMS:], g_sq[:, :], 0.0, EPS_GN, ALU.max, ALU.add).then_inc(gn_step, 1)

            def normalise(t):
                if t is None:
                    return
                dve.wait_ge(newton_step, t.count(6, 3))
                nc.vector.scalar_tensor_tensor(out=g_off[:, :], in0=g_mom[:, :, 0], scalar=-1.0, in1=inv_root[:, NORMS:], op0=ALU.mult, op1=ALU.mult).then_inc(gn_step, 1)
                dve.wait_ge(gn_step, t.count(GN_OPS, GN_OPS))
                past(dve, v_done, t.count(2, -2))
                for c in range(CC):
                    nc.vector.tensor_scalar(xn[:, t.parity, c, :], x_all[:, bass.ds(t.image, 1), c, :].rearrange("p o t -> p (o t)"),
                                            inv_root[:, NORMS + c:NORMS + c + 1], g_off[:, c:c + 1], ALU.mult, ALU.add).then_inc(xn_ready, 1)

            def sum_norms(t, e):
                if t is None:
                    return
                dve.wait_ge(squared, t.count(2, e + 1))
                nc.vector.tensor_reduce(sums[:, 0:NORMS], squares[:, :].rearrange("p (h d) -> p h d", d=HD), AX_X, ALU.add).then_inc(norms_summed, 1)

            def roots(j, base, e, n):
                at = root_columns(job(j, base, 0), job(j, base, 1) if e else None)
                if at is None:
                    return
                y, v, tmp = inv_root[:, at], sums[:, at], newton[:, at]
                if n == 0:
                    dve.wait_ge(seeded, base.count(2, e + 2))
                    nc.vector.tensor_tensor(tmp, y, y, ALU.mult).then_inc(newton_step, 1)
                else:
                    dve.wait_ge(newton_step, base.count(6, 3 * e + 3 + n))
                if n == 1:
                    nc.vector.scalar_tensor_tensor(out=tmp, in0=tmp, scalar=-0.5, in1=v, op0=ALU.mult, op1=ALU.mult).then_inc(newton_step, 1)
                if n == 2:
                    nc.vector.scalar_tensor_tensor(out=y, in0=tmp, scalar=1.5, in1=y, op0=ALU.add, op1=ALU.mult).then_inc(newton_step, 1)

            def scale_norms(t, e):
                if t is None:
                    return
                dve.wait_ge(newton_step, t.count(6, 3 * e + 6))
                nc.vector.scalar_tensor_tensor(out=rnorm[:, :], in0=inv_root[:, 0:NORMS], scalar=INV_NORM_TOP, in1=qk_scale[:, t.layer, :],
                                               op0=ALU.min, op1=ALU.mult).then_inc(rnorm_ready, 1)

            def make_unit(t, e):
                if t is None:
                    return
                dve.wait_ge(rnorm_ready, t.count(2, e + 1))
                past(dve, lo_ready, t.count(4, 2 * e))
                nc.vector.tensor_tensor(unit[:, :].rearrange("p (h d) -> p h d", d=HD), b_qk[e][:, :].rearrange("p (h d) -> p h d", d=HD),
                                        rnorm[:, :].rearrange("p (h o) -> p h o", o=1).broadcast_to([P, NORMS, HD]), ALU.mult).then_inc(unit_ready, 1)

            def keep_k(t, e):
                if t is None:
                    return
                T = t.count(2, e + 1)
                dve.wait_ge(k_turned, T)
                past(dve, scored, t.count(4, 2 * e - 2))
                nc.vector.tensor_copy(k_rows[N:P, e, :, :, N:P].rearrange("p w g m -> p g w m"),
                                      turned[N:P, :, :].rearrange("p g (w m) -> p g w m", w=2)).then_inc(k_ready1, 1)

            def invert_sums(t, e):
                if t is None:
                    return
                dve.wait_ge(mix_done, t.count(2, e + 1))
                past(dve, sums_spread, t.count(8, 4 * e))
                nc.vector.reciprocal(inv_sums[:, :], sum_rows[e]).then_inc(sums_inverted, 1)

            def spread_sums(t, e):
                if t is None:
                    return
                dve.wait_ge(sums_inverted, t.count(2, e + 1))
                past(dve, mixed_ready, t.count(2, e))
                past(dve, sums_seen, t.count(2, e))
                nc.vector.tensor_tensor(top_inverse[:, :], top_inverse[:, :], inv_sums[:, :], ALU.max).then_inc(sums_seen, 1)
                for w in range(2):
                    for c in range(CC):
                        nc.vector.stream_shuffle(r_sum[:, c, w * N:(w + 1) * N], inv_sums[:, :],
                                                 [4 * w + 2 * c + p // HD for p in range(32)]).then_inc(sums_spread, 1)

            def divide(t, e):
                if t is None:
                    return
                dve.wait_ge(sums_spread, t.count(8, 4 * e + 4))
                past(dve, z_done, t.count(2, e - 1))
                nc.vector.tensor_tensor(mixed[:, e, :, :], mix_cols[e], r_sum[:, :, :], ALU.mult).then_inc(mixed_ready, 1)

            def add_residual(t, e):
                if t is None:
                    return
                dve.wait_ge(z_done, t.count(2, e + 1))
                if t.layer and e == 0:
                    past(dve, out_stored[t.parity], 16 * t.half - 8 * IMAGES)
                for c in range(CC):
                    at = slice(e * P, (e + 1) * P)
                    here = x_all[:, bass.ds(t.image, 1), c, at].rearrange("p o t -> p (o t)")
                    ins = nc.vector.scalar_tensor_tensor(out=x_out[:, t.parity, c, at] if t.layer else here, in0=z_cols[:, c, :],
                                                         scalar=out_bias[:, t.layer, c:c + 1], in1=here, op0=ALU.add, op1=ALU.add)
                ins.then_inc(x_updated, 1)

            def iteration(j, base):
                after = job(j, base, 1)
                for e in range(2):
                    g = after if e == 1 else None
                    group_variance(g, 0)
                    invert_sums(*tile(j, base, e, 5))
                    group_variance(g, 1)
                    spread_sums(*tile(j, base, e, 5))
                    group_variance(g, 2)
                    divide(*tile(j, base, e, 5))
                    group_variance(g, 3)
                    if e == 0:
                        group_moments(after)
                    sum_norms(*tile(j, base, e, 0))
                    add_residual(*tile(j, base, e, 5))
                    keep_k(*tile(j, base, e, 2))
                    for n in range(3):
                        roots(j, base, e, n)
                    scale_norms(*tile(j, base, e, 0))
                    make_unit(*tile(j, base, e, 0))
                    if e == 1:
                        normalise(after)

            run(dve, iteration)

        @block.gpsimd
        def _(pool):
            nc.gpsimd.memset(q_aug[:, :, :, :, :], 0.0).then_inc(su_pool, 1)
            nc.gpsimd.memset(top_inverse[:, :], 0.0).then_inc(su_pool, 1)
            nc.gpsimd.memset(k_aug[:, :, :, :], 0.0).then_inc(aug_zero, 1)
            nc.gpsimd.memset(k_rows[:, :, :, :, :], 0.0).then_inc(aug_zero, 1)
            nc.gpsimd.memset(v_pair[:, :, :, :, :], 0.0).then_inc(aug_zero, 1)
            pool.wait_ge(aug_zero, 3)
            pool.wait_ge(su_pool, 1)
            nc.gpsimd.memset(k_aug[:, :, :, 3 * HD:3 * HD + 2], 1.0).then_inc(aug_zero, 1)
            pool.wait_ge(aug_zero, 4)

            def split_lo(t, e):
                if t is None:
                    return
                pool.wait_ge(hi_ready, t.count(4, 2 * e + 2))
                for n, dst, hi in ((0, q_aug[:, t.layer, e, :, 2 * HD:3 * HD], q_aug[:, t.layer, e, :, 0:HD]),
                                   (1, k_aug[:, e, :, HD:2 * HD], k_aug[:, e, :, 0:HD])):
                    nc.gpsimd.tensor_tensor(dst, unit[:, n * D:(n + 1) * D].rearrange("p (h d) -> p h d", d=HD), hi, ALU.subtract).then_inc(lo_ready, 1)

            def weigh(t, e):
                if t is None:
                    return
                for w in range(2):
                    pool.wait_ge(exped, t.count(4, 2 * e + w + 1))
                    pr = probs[:, 2 * e + w, :, :]
                    nc.gpsimd.tensor_tensor(pr, pr, exp_bias[:, t.layer, 2 * e + w, :, :], ALU.mult).then_inc(weighted, 1)

            pool.wait_ge(su_dve, SU_DVE_PER_LAYER * LAYERS)

            def iteration(j, base):
                for e in range(2):
                    split_lo(*tile(j, base, e, 1))
                    weigh(*tile(j, base, e, 3))

            run(pool, iteration)


_WEIGHTS = ['Wq', 'Wk', 'Wv', 'bv', 'Wo', 'bo', 'logit_scale', 'cpb_w1', 'cpb_b1', 'cpb_w2']


def _constants():
    import numpy as np
    group = D // 32
    r = np.arange(-(WIN - 1), WIN, dtype=np.float32)
    t = np.stack(np.meshgrid(r, r, indexing="ij"), axis=-1) / (WIN - 1) * 8.0
    t = np.sign(t) * np.log2(np.abs(t) + 1.0) / 3.0
    t = t.reshape(-1, 2)[::-1].T
    pos = np.arange(N)
    low_r, low_c = pos // WIN < WIN - SHIFT, pos % WIN < WIN - SHIFT
    same = [np.ones((N, N), bool), low_c[:, None] == low_c[None, :], low_r[:, None] == low_r[None, :]]
    same.append(same[1] & same[2])
    return {
        "ident16": np.eye(P, dtype=np.float16),
        "group_mean": np.kron(np.eye(P // group), np.full((group, group), 0.5 / group)).astype(np.float32),
        "coords": np.concatenate([t, np.ones((1, REL * REL))]).astype(np.float32),
        "sum_cols": np.stack([np.kron(np.eye(2), np.ones((N, 1))) @ np.tile(np.eye(8)[2 * i:2 * i + 2], 4) for i in range(4)], 1).astype(np.float32),
        "act_bias": np.tile(np.float32([-BIAS_MID, LN_SCALE * LN_FLOOR, 0.5 * math.log(LN_SCALE)]), (P, 1)),
        "masks": np.stack(same).astype(np.float32),
    }


def _to_channels(x):
    import numpy as np
    x = np.roll(x, (-SHIFT, -SHIFT), axis=(1, 2))
    x = x.reshape(IMAGES, SIDE // WIN, WIN, SIDE // WIN, WIN, CC, P)
    return x.transpose(6, 0, 5, 1, 3, 2, 4).reshape(P, IMAGES, CC, TOKENS)


def _from_channels(y):
    import numpy as np
    y = y.reshape(P, IMAGES, CC, SIDE // WIN, SIDE // WIN, WIN, WIN)
    y = y.transpose(1, 3, 5, 4, 6, 2, 0).reshape(IMAGES, SIDE, SIDE, D)
    return np.roll(y, (SHIFT, SHIFT), axis=(1, 2))


def kernel(**inputs):
    import numpy as _np
    import concourse.bacc as _bacc
    from concourse import mybir as _mybir
    from concourse.bass_utils import run_bass_kernel_spmd as _run

    nc = _bacc.Bacc("TRN2", target_bir_lowering=False, num_devices=1)
    arrays = {}

    def put(name, a):
        a = _np.ascontiguousarray(a)
        arrays[name] = a
        return nc.dram_tensor(name, a.shape, _mybir.dt.from_np(a.dtype), kind="ExternalInput").ap()

    x = put("in_x", _to_channels(_np.asarray(inputs["x"])))
    weights = []
    for l in range(LAYERS):
        w = {n: _np.asarray(inputs[f"L{l}_conv_{n}"]) for n in _WEIGHTS}
        weights.append({n: put(f"in_L{l}_{n}", a.T if a.ndim == 2 else a) for n, a in w.items()})
    consts = {name: put(f"const_{name}", a) for name, a in _constants().items()}
    scratch = nc.dram_tensor("table_scratch", (LAYERS, HEADS, REL * REL), F32, kind="Internal").ap()
    out = nc.dram_tensor("out_0", (P, IMAGES, CC, TOKENS), F32, kind="ExternalOutput").ap()
    build(nc, x, weights, out, consts, scratch)
    r = _run(nc, [arrays], core_ids=[0])
    return _from_channels(r.results[0]["out_0"])
```

```python
import math
from contextlib import ExitStack

import concourse.bass as bass
from concourse import mybir

F32 = mybir.dt.float32
F32R = mybir.dt.float32r
F16 = mybir.dt.float16
I32 = mybir.dt.int32
ALU = mybir.AluOpType
ACT = mybir.ActivationFunctionType
AX_X = mybir.AxisListType.X

P = 128
IMAGES, SIDE, D = 32, 16, 256
LAYERS = 2
WIN, SHIFT, HEADS = 8, 4, 16
N = WIN * WIN
HD = D // HEADS
PAIRS = HEADS // 2
CC = D // P
TOKENS = SIDE * SIDE
TILES = TOKENS // P
REL = 2 * WIN - 1
STEPS_BACK = 3
RUN = (WIN - 1) * REL + WIN
AUG = 64
NORMS = 2 * HEADS
JOBS = LAYERS * IMAGES
BIAS_TOP = 16.0
BIAS_MID = BIAS_TOP / 2
HEADROOM = 75.0
LOG100 = 4.605170185988092
EPS_GN = 1e-5
INV_NORM_TOP = 1e12
LN_SCALE = 2.0 ** 32
LN_FLOOR = 1e-28
INVERSE_TOP = math.exp(57.0)
INVERSE_CAP = 1e37
CONST_COLS = {"group_mean": P, "sum_cols": 4 * 32, "act_bias": 4, "hide": 2 * N, "masks": 4 * N}
HIDDEN = -1e4


class Job:

    def __init__(self, half, parity, layer, exact):
        self.half, self.parity, self.layer, self.exact = half, parity, layer, exact

    def __add__(self, k):
        s = self.parity + k
        return Job(self.half + s // 2, s % 2, self.layer, self.exact)

    def count(self, per_image, done):
        return 2 * per_image * self.half + (per_image * self.parity + done)

    def count_exact(self, per_image, done):
        return self.count(per_image, done - per_image * JOBS)

    def loads(self, step):
        return step * self.half - step * self.exact * (IMAGES // 2)

    def stores(self, step):
        return step * self.half - step * (1 + self.exact) * (IMAGES // 2)

    @property
    def image(self):
        return 2 * self.half + (self.parity - IMAGES * (self.layer + LAYERS * self.exact))


def build(nc, x, weights, out, consts, table_scratch):
    with ExitStack() as ctx:
        def sb(name, shape, dt=F32):
            return ctx.enter_context(nc.sbuf_tensor(name, shape, dt))

        def sem(name):
            return ctx.enter_context(nc.semaphore(name))

        L = LAYERS
        ident16 = sb("ident16", [P, P], F16)
        consts32 = sb("consts32", [P, sum(CONST_COLS.values())])
        at, views = 0, {}
        for name, cols in CONST_COLS.items():
            views[name] = consts32[:, at:at + cols]
            at += cols
        group_mean = views["group_mean"]
        coords = sb("coords", [3, REL * REL])
        masks = views["masks"].rearrange("p (w n) -> p w n", n=N)
        sum_cols = views["sum_cols"].rearrange("p (i k) -> p i k", k=32)
        act_bias = views["act_bias"]
        hide = views["hide"].rearrange("p (e m) -> p e m", m=N)
        w_qk = sb("w_qk", [P, 2, L, CC, 2 * D], F32R)
        w_v = sb("w_v", [P, 2, L, CC, D], F32R)
        w_o = sb("w_o", [P, L, CC, D])
        biases = sb("biases", [P, L, 2, CC])
        out_bias = sb("out_bias", [P, L, CC])
        cpb1 = sb("cpb1", [3, L, P])
        cpb2 = sb("cpb2", [P, L, HEADS])
        hidden = sb("hidden", [P, L, REL * REL])
        table = sb("table", [HEADS, L, REL * REL])
        bias_rev = sb("bias_rev", [P, L, PAIRS, WIN * REL])
        exp_bias = sb("exp_bias", [P, L, 4, PAIRS, N])
        qk_scale = sb("qk_scale", [P, L, 2 * HEADS])
        shift32 = sb("shift32", [P, L, HEADS])

        x_all = sb("x_all", [P, IMAGES, CC, TOKENS])
        bn6 = sb("bn6", [P, CC, 2, 3])
        mean_sq = sb("mean_sq", [P, CC, 2])
        g_mom = sb("g_mom", [P, CC, 2])
        g_sq = sb("g_sq", [P, CC])
        g_off = sb("g_off", [P, CC])
        xn32 = sb("xn32", [P, CC, TOKENS])
        xn = sb("xn", [P, 2, 2, CC, TOKENS], F32R)
        squares = sb("squares", [P, 2 * D])
        sums = sb("sums", [P, NORMS + CC])
        logs = sb("logs", [P, NORMS + CC])
        newton = sb("newton", [P, NORMS + CC])
        inv_root = sb("inv_root", [P, NORMS + CC])
        rnorm = sb("rnorm", [P, NORMS])
        unit = sb("unit", [P, 2 * D])
        q_aug = sb("q_aug", [P, L, 2, HEADS, AUG], F16)
        k_aug = sb("k_aug", [P, 2, HEADS, AUG], F16)
        q_rows = sb("q_rows", [P, 2, PAIRS, P], F16)
        k_rows = sb("k_rows", [P, 2, 2, PAIRS, P], F16)
        v_pair = sb("v_pair", [P, 4, 2, PAIRS, 32])
        probs = sb("probs", [P, 4, PAIRS, N])
        inv_sums = sb("inv_sums", [P, N])
        top_inverse = sb("top_inverse", [P, N])
        lost = sb("lost", [P, 1])
        flag = sb("flag", [1, 1], I32)
        allowed = sb("allowed", [P, PAIRS, N])
        row_max = sb("row_max", [P, HEADS])
        row_shift = sb("row_shift", [P, HEADS])
        r_sum = sb("r_sum", [P, CC, P])
        mixed = sb("mixed", [P, 2, CC, P])
        x_out = sb("x_out", [P, 2, CC, TOKENS])

        w_qk_in = probs[:, :, :, :].rearrange("p (l c) (a g) n -> p l c (a g n)", l=L, a=1)
        w_v_in = x_out[:, :, :, :]

        ps = [ctx.enter_context(nc.psum_tensor(f"bank{i}", [P, 512], F32)) for i in range(8)]
        b_qk, b_turn, b_score, b_mix = ps[0:2], ps[2], ps[4:6], ps[6:8]
        v_cols = ps[3][:, 0:D]
        z_cols = ps[3][:, 0:CC * P].rearrange("p (c t) -> p c t", c=CC)
        g_cols = ps[3][:, 0:2 * CC]
        mix_cols = [b[:, 0:CC * P].rearrange("p (c t) -> p c t", c=CC) for b in b_mix]
        sum_rows = [b[:, CC * P:CC * P + N] for b in b_mix]
        turned = b_turn[:, :].bitcast(F16).rearrange("p (g t) -> p g t", g=PAIRS)

        consts_in = sem("consts_in")
        weights_in = [sem("weights_in0"), sem("weights_in1")]
        su_pe, su_act, su_dve, su_pool = sem("su_pe"), sem("su_act"), sem("su_dve"), sem("su_pool")
        table_out, bias_in = sem("table_out"), [sem("bias_in0"), sem("bias_in1")]
        x_loaded = [sem("x_loaded0"), sem("x_loaded1")]
        bn_step = sem("bn_step")
        aug_zero = sem("aug_zero")
        group_summed = sem("group_summed")
        gn_step = sem("gn_step")
        logged, seeded, newton_step = sem("logged"), sem("seeded"), sem("newton_step")
        w_hi, w_split, bias_ready = sem("w_hi"), sem("w_split"), sem("bias_ready")
        xn32_ready, xn_hi, xn_ready = sem("xn32_ready"), sem("xn_hi"), sem("xn_ready")
        qk_done, v_done = sem("qk_done"), sem("v_done")
        v_ready = sem("v_ready")
        squared = sem("squared")
        norms_summed, rnorm_ready = sem("norms_summed"), sem("rnorm_ready")
        unit_ready = sem("unit_ready")
        hi_ready, hi_again, lo_ready = sem("hi_ready"), sem("hi_again"), sem("lo_ready")
        q_turned, k_turned = sem("q_turned"), sem("k_turned")
        q_ready, k_ready0, k_ready1 = sem("q_ready"), sem("k_ready0"), sem("k_ready1")
        scored, exped, weighted = sem("scored"), sem("exped"), sem("weighted")
        mix_done, sums_inverted, sums_spread, mixed_ready = sem("mix_done"), sem("sums_inverted"), sem("sums_spread"), sem("mixed_ready")
        sums_seen = sem("sums_seen")
        q_scored, shift_set, shift_step = sem("q_scored"), sem("shift_set"), sem("shift_step")
        q_turned_again, q_refined, capped = sem("q_turned_again"), sem("q_refined"), sem("capped")
        flag_step, flag_summed, flag_ready = sem("flag_step"), sem("flag_summed"), sem("flag_ready")
        z_done, x_updated = sem("z_done"), sem("x_updated")
        out_stored = [sem("out_stored0"), sem("out_stored1")]

        CONSTS = 3
        PER_LAYER_IN = 7
        GATHERS = 2 * WIN
        BN_OPS, GN_OPS = CC + 2, 5
        SU_ACT_PER_LAYER, SU_DVE_PER_LAYER = 4, 10
        SU_POOL = 2

        def past(engine, semaphore, value):
            if not (isinstance(value, int) and value <= 0):
                engine.wait_ge(semaphore, value)

        def run(engine, iteration, exact):
            def some(a, b):
                for j in range(a, b):
                    half, parity = divmod(j + JOBS * exact, 2)
                    iteration(j, Job(half, parity, None, exact))

            some(-2, 6)
            for layer in range(LAYERS):
                first = IMAGES * layer + 6
                last = IMAGES * (layer + 1) - 4
                with engine.Fori((first + JOBS * exact) // 2, (last + JOBS * exact) // 2) as half:
                    for parity in range(2):
                        iteration(first + parity, Job(half, parity, None, exact))
                some(last, last + (10 if layer + 1 < LAYERS else 4 + STEPS_BACK))

        def both_passes(engine, iteration, between=None):
            run(engine, iteration, 0)
            if between is not None:
                between()
            engine.wait_ge(flag_ready, 1)
            again = engine.value_load(flag[0:1, 0:1], min_val=0, max_val=P)
            with engine.If(again != 0):
                run(engine, iteration, 1)

        def tile(j, base, e, back):
            k = (e - back) // 2
            return job(j, base, k), e - back - 2 * k

        def job(j, base, k):
            if not 0 <= j + k < JOBS:
                return None
            got = base + k
            got.layer = (j + k) // IMAGES
            return got

        def root_columns(t, after):
            if t is None and after is None:
                return None
            return slice(0 if t is not None else NORMS, NORMS + CC if after is not None else NORMS)

        def rooted(j, base, e, done=0, ops=1):
            if j < 0:
                return ops * (2 * JOBS + 1) * base.exact + done
            return base.count(2 * ops, ops * (e + 1 + base.exact) + done)

        block = ctx.enter_context(nc.Block())

        @block.sync
        def _(sp):
            def load_x(t):
                if t is None or t.layer:
                    return
                past(sp, x_loaded[t.parity], t.loads(16))
                sp.dma_start(x_all[:, bass.ds(t.image, 1), :, :], x[:, bass.ds(t.image, 1), :, :]).then_inc(x_loaded[t.parity], 16)

            def store_x(t):
                if t is None or t.layer == 0:
                    return
                sp.wait_ge(x_updated, t.count(2, 2))
                sp.dma_start(out[:, bass.ds(t.image, 1), :, :], x_out[:, t.parity:t.parity + 1, :, :]).then_inc(out_stored[t.parity], 16)

            def load_weights(l):
                w = weights[l]
                matrices = w["matrices"].rearrange("(c p) o -> p c o", p=P)
                for dst, src in ((cpb1[:, l, :], w["cpb1"]), (cpb2[:, l, :], w["cpb2"]),
                                 (qk_scale[:, l, 0:HEADS], w["logit_scale"].rearrange("(o h) -> o h", o=1).broadcast_to([P, HEADS])),
                                 (w_qk_in[:, l, :, :], matrices[:, :, 0:2 * D]), (w_v_in[:, l, :, :], matrices[:, :, 2 * D:3 * D]),
                                 (w_o[:, l, :, :], matrices[:, :, 3 * D:]), (biases[:, l, :, :], w["biases"])):
                    sp.dma_start(dst, src).then_inc(weights_in[l], 16)

            for dst, name in ((consts32[:, :], "consts32"), (coords[:, :], "coords"), (ident16[:, :], "ident16")):
                sp.dma_start(dst, consts[name]).then_inc(consts_in, 16)
            load_weights(0)
            load_x(Job(0, 0, 0, 0))
            load_weights(1)
            def spread_bias(l):
                sp.wait_ge(su_act, SU_ACT_PER_LAYER * (l + 1))
                sp.dma_start(table_scratch[l], table[:, l, :]).then_inc(table_out, 16)
                sp.wait_ge(table_out, 16 * (l + 1))
                for a in range(2):
                    for rm in range(WIN):
                        at = table_scratch[l, a, rm * REL:]
                        src = bass.AP(at.tensor, at.offset, [[1, WIN], [2 * REL * REL, PAIRS], [1, RUN]])
                        p0 = N * a + WIN * rm
                        sp.dma_start(bias_rev[p0:p0 + WIN, l, :, 0:RUN], src).then_inc(bias_in[l], 16)

            spread_bias(0)

            def iteration(j, base):
                if j == -2 and base.exact:
                    load_x(job(j, base, 2))
                load_x(job(j, base, 3))
                if j == 0 and not base.exact:
                    spread_bias(1)
                store_x(job(j, base, -3))
                if j == JOBS + 2:
                    for parity in range(2):
                        sp.wait_ge(out_stored[parity], 16 * (1 + base.exact) * IMAGES // 2)

            both_passes(sp, iteration)

        @block.tensor
        def _(pe):
            pe.wait_ge(consts_in, 16 * CONSTS)
            for l in range(LAYERS):
                pe.wait_ge(weights_in[l], 16 * PER_LAYER_IN)
                for c in range(CC):
                    for k in range(CC):
                        last = nc.tensor.matmul(ps[l][:, c:c + 1], w_o[:, l, k, c * P:(c + 1) * P], biases[:, l, 0, k:k + 1],
                                                start=(k == 0), stop=(k == CC - 1))
                last.then_inc(su_pe, 1)
                nc.tensor.matmul(ps[4 + l][:, 0:REL * REL], cpb1[:, l, :], coords[:, :], start=True, stop=True)\
                    .then_inc(su_pe, 1)
            for l in range(LAYERS):
                pe.wait_ge(su_act, SU_ACT_PER_LAYER * l + 1)
                nc.tensor.matmul(ps[6 + l][0:HEADS, 0:REL * REL], cpb2[:, l, :], hidden[:, l, :], start=True, stop=True)\
                    .then_inc(su_pe, 1)
            pe.wait_ge(su_act, SU_ACT_PER_LAYER * LAYERS)
            pe.wait_ge(su_dve, SU_DVE_PER_LAYER * LAYERS)
            pe.wait_ge(su_pool, SU_POOL)
            pe.wait_ge(aug_zero, 4)
            pe.wait_ge(w_split, 2 * LAYERS)

            PARTS = ((0, 0), (0, 1), (1, 0))

            def sum_groups(t):
                if t is None:
                    return
                past(pe, v_ready, t.count(8, -8))
                pe.wait_ge(bn_step, t.count(BN_OPS, BN_OPS))
                for s in range(2):
                    last = nc.tensor.matmul(g_cols, group_mean[:, :], bn6[:, :, s, 1:3], start=(s == 0), stop=(s == 1), skip_group_check=True)
                last.then_inc(group_summed, 1)

            def project_qk(t, e):
                if t is None:
                    return
                if e == 0:
                    pe.wait_ge(xn_ready, t.count(1, 1))
                past(pe, unit_ready, t.count(2, e - 1))
                for c in range(CC):
                    for i, (px, pw) in enumerate(PARTS):
                        last = nc.tensor.matmul(b_qk[e][:, :], xn[:, px, t.parity, c, e * P:(e + 1) * P], w_qk[:, pw, t.layer, c, :],
                                                start=(c == 0 and i == 0), stop=(c == CC - 1 and i == len(PARTS) - 1))
                last.then_inc(qk_done, 1)

            def project_v(t, e, after):
                if t is None:
                    return
                if after is not None:
                    pe.wait_ge(gn_step, after.count(GN_OPS, 1))
                past(pe, v_ready, t.count(8, 4 * e))
                past(pe, x_updated, t.count(2, e - 4))
                for c in range(CC):
                    for i, (px, pw) in enumerate(PARTS):
                        last = nc.tensor.matmul(v_cols, xn[:, px, t.parity, c, e * P:(e + 1) * P], w_v[:, pw, t.layer, c, :],
                                                start=(c == 0 and i == 0), stop=(c == CC - 1 and i == len(PARTS) - 1), skip_group_check=True)
                last.then_inc(v_done, 1)

            def turn_q(t, e):
                if t is None:
                    return
                T1 = t.count(2, e)
                pe.wait_ge(hi_again, t.count(4, 2 * e + 2))
                pe.wait_ge(lo_ready, t.count(4, 2 * e + 2))
                past(pe, k_ready0, T1)
                past(pe, k_ready1, T1)
                if t.exact:
                    past(pe, q_refined, t.count_exact(2, e))
                    pe.wait_ge(shift_set, t.count_exact(4, 2 * e + 2))
                for g in range(PAIRS):
                    last = nc.tensor.transpose(turned[:, g, :], q_aug[:, t.layer, e, 2 * g:2 * g + 2, :].rearrange("p a r -> p (a r)"), ident16[:, :])
                last.then_inc(q_turned, 1)

            def turn_k(t, e):
                if t is None:
                    return
                pe.wait_ge(q_ready, t.count(2, e + 1))
                for g in range(PAIRS):
                    last = nc.tensor.transpose(turned[:, g, :], k_aug[:, e, 2 * g:2 * g + 2, :].rearrange("p a r -> p (a r)"), ident16[:, :])
                last.then_inc(k_turned, 1)

            def score(t, e):
                if t is None:
                    return
                T = t.count(2, e + 1)
                pe.wait_ge(q_ready, T)
                pe.wait_ge(k_ready0, T)
                pe.wait_ge(k_ready1, T)
                if t.exact:
                    pe.wait_ge(q_refined, t.count_exact(2, e + 1))
                for w in range(2):
                    past(pe, exped, t.count(4, 2 * e + w - 1))
                    for g in range(PAIRS):
                        last = nc.tensor.matmul(b_score[w][:, g * N:(g + 1) * N], k_rows[:, e, w, g, :],
                                                q_rows[:, e, g, w * N:(w + 1) * N], start=True, stop=True, skip_group_check=True)
                    last.then_inc(scored, 1)

            def refine(t, e):
                if t is None or not t.exact:
                    return
                T = t.count(2, e + 1)
                pe.wait_ge(q_ready, T)
                pe.wait_ge(k_ready0, T)
                pe.wait_ge(k_ready1, T)
                pe.wait_ge(exped, t.count(4, 2 * e))
                for g in range(PAIRS):
                    for w in range(2):
                        last = nc.tensor.matmul(b_score[g // 4][N * w:N * w + N, (g % 4) * P:(g % 4 + 1) * P], q_rows[:, e, g, w * N:(w + 1) * N],
                                                k_rows[:, e, w, g, :], start=True, stop=True, skip_group_check=True)
                last.then_inc(q_scored, 1)
                pe.wait_ge(shift_step, t.count_exact(16, 8 * e + 8))
                for g in range(PAIRS):
                    last = nc.tensor.transpose(turned[:, g, :], q_aug[:, t.layer, e, 2 * g:2 * g + 2, :].rearrange("p a r -> p (a r)"), ident16[:, :])
                last.then_inc(q_turned_again, 1)

            def mix(t, e):
                if t is None:
                    return
                past(pe, mixed_ready, t.count(2, e - 1))
                pe.wait_ge(v_ready, t.count(8, 4 * e + 4))
                vb = 2 * t.parity + e
                for w in range(2):
                    pe.wait_ge(weighted, t.count(4, 2 * e + w + 1))
                    for g in range(PAIRS):
                        c, r = divmod(g, 4)
                        nc.tensor.matmul(mix_cols[e][32 * r:32 * r + 32, c, w * N:(w + 1) * N], v_pair[:, vb, w, g, :],
                                         probs[:, 2 * e + w, g, :], start=True, stop=True, skip_group_check=True)
                for w in range(2):
                    for c in range(CC):
                        for r in range(4):
                            last = nc.tensor.matmul(sum_rows[e][32 * r:32 * r + 32, :], sum_cols[:, 2 * w + c, :], probs[:, 2 * e + w, 4 * c + r, :],
                                                    start=(w == 0 and c == 0), stop=(w == 1 and c == CC - 1), skip_group_check=True)
                last.then_inc(mix_done, 1)

            def project_out(t, e, after, newest, newest_e):
                if t is None:
                    return
                pe.wait_ge(mixed_ready, t.count(2, e + 1))
                if after is not None:
                    pe.wait_ge(gn_step, after.count(GN_OPS, 1))
                if newest is not None:
                    pe.wait_ge(v_ready, newest.count(8, 4 * newest_e + 4))
                else:
                    pe.wait_ge(x_updated, t.count(2, e))
                for c in range(CC):
                    for k in range(CC):
                        last = nc.tensor.matmul(z_cols[:, c, :], w_o[:, t.layer, k, c * P:(c + 1) * P], mixed[:, e, k, :],
                                                start=(k == 0), stop=(k == CC - 1), skip_group_check=True)
                last.then_inc(z_done, 1)

            def iteration(j, base):
                for e in range(2):
                    after = job(j, base, 1) if e == 0 else None
                    turn_q(*tile(j, base, e, 2))
                    project_qk(*tile(j, base, e, 0))
                    sum_groups(after)
                    turn_k(*tile(j, base, e, 2))
                    project_out(*tile(j, base, e, 5), after, *tile(j, base, e, 1))
                    mix(*tile(j, base, e, 4))
                    score(*tile(j, base, e, 3))
                    refine(*tile(j, base, e, 2))
                    project_v(*tile(j, base, e, 0), after)

            def sum_lost():
                pe.wait_ge(flag_step, 2)
                nc.tensor.matmul(ps[3][0:1, 0:1], lost[:, :], act_bias[:, 3:4], start=True, stop=True).then_inc(flag_summed, 1)

            both_passes(pe, iteration, sum_lost)

        @block.scalar
        def _(act):
            nc.scalar.preload_act_table_set("natural_log_exp_and_others")
            act.wait_ge(consts_in, 16 * CONSTS)
            for l in range(LAYERS):
                act.wait_ge(weights_in[l], 16 * PER_LAYER_IN)
                nc.scalar.activation(w_qk[:, 0, l, :, :], w_qk_in[:, l, :, :], ACT.Copy).then_inc(w_hi, 1)
                nc.scalar.activation(w_v[:, 0, l, :, :], w_v_in[:, l, :, :], ACT.Copy).then_inc(w_hi, 1)
                act.wait_ge(su_pe, 2 * l + 2)
                nc.scalar.activation(hidden[:, l, :], ps[4 + l][:, 0:REL * REL], ACT.Relu).then_inc(su_act, 1)
                act.wait_ge(su_dve, SU_DVE_PER_LAYER * l + 1)
                nc.scalar.activation(qk_scale[:, l, 0:HEADS], qk_scale[:, l, 0:HEADS], ACT.Exp).then_inc(su_act, 1)
                act.wait_ge(su_pe, 2 * LAYERS + l + 1)
                nc.scalar.activation(table[:, l, :], ps[6 + l][0:HEADS, 0:REL * REL], ACT.Exp, scale=-1.0).then_inc(su_act, 1)
                act.wait_ge(su_dve, SU_DVE_PER_LAYER * l + 8)
                nc.scalar.activation(table[:, l, :], table[:, l, :], ACT.Exp, bias=act_bias[0:HEADS, 0:1], scale=BIAS_TOP).then_inc(su_act, 1)

            def keep_q(t, e):
                if t is None:
                    return
                T = t.count(2, e + 1)
                act.wait_ge(q_turned, T)
                past(act, scored, t.count(4, 2 * e - 2))
                nc.scalar.activation(q_rows[:, e, :, :], turned, ACT.Copy).then_inc(q_ready, 1)

            def keep_q_again(t, e):
                if t is None or not t.exact:
                    return
                act.wait_ge(q_turned_again, t.count_exact(2, e + 1))
                nc.scalar.activation(q_rows[:, e, :, :], turned, ACT.Copy).then_inc(q_refined, 1)

            def round_xn(t):
                if t is None:
                    return
                act.wait_ge(xn32_ready, t.count(2, 2))
                past(act, v_done, t.count(2, -2))
                nc.scalar.activation(xn[:, 0, t.parity, :, :], xn32[:, :, :], ACT.Copy).then_inc(xn_hi, 1)

            def keep_v(t, e):
                if t is None:
                    return
                T = t.count(2, e + 1)
                act.wait_ge(v_done, T)
                past(act, mix_done, t.count(2, e + 1 - 4))
                v = v_cols.rearrange("p (g a d) -> p g a d", g=PAIRS, a=2)
                for w in range(2):
                    for a in range(2):
                        nc.scalar.activation(v_pair[N * a:N * a + N, 2 * t.parity + e, w, :, HD * a:HD * a + HD],
                                             v[N * w:N * w + N, :, a, :], ACT.Copy).then_inc(v_ready, 1)

            def square(t, e):
                if t is None:
                    return
                act.wait_ge(qk_done, t.count(2, e + 1))
                past(act, norms_summed, t.count(2, e))
                nc.scalar.activation(squares[:, :], b_qk[e][:, :], ACT.Square).then_inc(squared, 1)

            def seed_roots(j, base, e):
                t, after = job(j, base, 0), job(j, base, 1) if e == 0 else None
                at = root_columns(t, after)
                if at is None:
                    return
                if t is not None:
                    act.wait_ge(norms_summed, t.count(2, e + 1))
                if after is not None:
                    act.wait_ge(gn_step, after.count(GN_OPS, 4))
                past(act, seeded, rooted(j, base, e))
                nc.scalar.activation(logs[:, at], sums[:, at], ACT.Ln, bias=act_bias[:, 1:2], scale=LN_SCALE).then_inc(logged, 1)
                act.wait_ge(logged, rooted(j, base, e, 1))
                past(act, rnorm_ready, t.count(2, e) if t is not None else 0)
                past(act, xn32_ready, base.count(2, 2) if after is not None else 0)
                nc.scalar.activation(inv_root[:, at], logs[:, at], ACT.Exp, bias=act_bias[:, 2:3], scale=-0.5).then_inc(seeded, 1)

            def keep_k(t, e):
                if t is None:
                    return
                T = t.count(2, e + 1)
                act.wait_ge(k_turned, T)
                past(act, scored, t.count(4, 2 * e - 2))
                nc.scalar.activation(k_rows[0:N, e, :, :, 0:N].rearrange("p w g m -> p g w m"),
                                     turned[0:N, :, :].rearrange("p g (w m) -> p g w m", w=2), ACT.Copy).then_inc(k_ready0, 1)

            def split_hi(t, e):
                if t is None:
                    return
                T = t.count(2, e + 1)
                act.wait_ge(unit_ready, T)
                past(act, k_turned, t.count(2, e - 1))
                for n, dst in enumerate((q_aug[:, t.layer, e, :, 0:HD], k_aug[:, e, :, 0:HD])):
                    nc.scalar.activation(dst, unit[:, n * D:(n + 1) * D].rearrange("p (h d) -> p h d", d=HD), ACT.Copy).then_inc(hi_ready, 1)

            def exp(t, e, w):
                if t is None:
                    return
                act.wait_ge(scored, t.count(4, 2 * e + w + 1))
                if t.exact:
                    act.wait_ge(capped, t.count_exact(4, 2 * e + w + 1))
                past(act, mix_done, t.count(2, e + 1 - 2))
                nc.scalar.activation(probs[:, 2 * e + w, :, :].rearrange("p g n -> p (g n)"), b_score[w][:, :], ACT.Exp).then_inc(exped, 1)

            def iteration(j, base):
                for e in range(2):
                    keep_v(*tile(j, base, e, 1))
                    keep_q(*tile(j, base, e, 2))
                    square(*tile(j, base, e, 0))
                    split_hi(*tile(j, base, e, 1))
                    if e == 1:
                        round_xn(job(j, base, 1))
                    seed_roots(j, base, e)
                    keep_k(*tile(j, base, e, 2))
                    exp(*tile(j, base, e, 3), 0)
                    exp(*tile(j, base, e, 3), 1)
                    keep_q_again(*tile(j, base, e, 2))

            both_passes(act, iteration)

        @block.vector
        def _(dve):
            dve.wait_ge(consts_in, 16 * CONSTS)
            for l in range(LAYERS):
                dve.wait_ge(weights_in[l], 16 * PER_LAYER_IN)
                b = SU_DVE_PER_LAYER * l
                nc.vector.tensor_scalar(qk_scale[:, l, 0:HEADS], qk_scale[:, l, 0:HEADS], LOG100, None, ALU.min).then_inc(su_dve, 1)
                nc.vector.memset(qk_scale[:, l, HEADS:2 * HEADS], 1.0).then_inc(su_dve, 1)
                dve.wait_ge(su_pe, 2 * l + 1)
                nc.vector.tensor_tensor(out_bias[:, l, :], ps[l][:, 0:CC], biases[:, l, 1, :], ALU.add).then_inc(su_dve, 1)
                dve.wait_ge(su_act, SU_ACT_PER_LAYER * l + 2)
                nc.vector.tensor_scalar(shift32[:, l, :], qk_scale[:, l, 0:HEADS], -1.0, HEADROOM, ALU.mult, ALU.add).then_inc(su_dve, 1)
                dve.wait_ge(su_dve, b + 4)
                dve.wait_ge(su_pool, 1)
                for e in range(2):
                    nc.vector.tensor_copy(q_aug[:, l, e, :, 3 * HD], shift32[:, l, :]).then_inc(su_dve, 1)
                for n, (parts, whole) in enumerate(((w_qk, w_qk_in), (w_v, w_v_in))):
                    dve.wait_ge(w_hi, 2 * l + n + 1)
                    nc.vector.tensor_tensor(parts[:, 1, l, :, :], whole[:, l, :, :], parts[:, 0, l, :, :], ALU.subtract).then_inc(w_split, 1)
                dve.wait_ge(su_act, SU_ACT_PER_LAYER * l + 3)
                nc.vector.tensor_scalar(table[:, l, :], table[:, l, :], 1.0, None, ALU.add).then_inc(su_dve, 1)
                dve.wait_ge(su_dve, b + 7)
                nc.vector.reciprocal(table[:, l, :], table[:, l, :]).then_inc(su_dve, 1)
                for e in range(2):
                    nc.vector.tensor_tensor(q_aug[:, l, e, :, 3 * HD + 1], shift32[:, l, :], q_aug[:, l, e, :, 3 * HD], ALU.subtract).then_inc(su_dve, 1)
            def mask_bias(l):
                dve.wait_ge(bias_in[l], 16 * GATHERS)
                rows = bias_rev[:, l, :, :].rearrange("p g (r c) -> p g r c", c=REL)[:, :, ::-1, WIN - 1::-1]
                for w in range(4):
                    nc.vector.tensor_tensor(exp_bias[:, l, w, :, :].rearrange("p g (r c) -> p g r c", c=WIN), rows,
                                            masks[:, w, :].rearrange("p (o r c) -> p o r c", o=1, c=WIN).broadcast_to([P, PAIRS, WIN, WIN]),
                                            ALU.mult).then_inc(bias_ready, 1)

            def group_moments(t):
                if t is None:
                    return
                if t.layer == 0:
                    dve.wait_ge(x_loaded[t.parity], t.loads(16) + 16)
                else:
                    dve.wait_ge(x_updated, t.count(2, 2 - 2 * IMAGES))
                past(dve, group_summed, t.count(1, 0))
                for c in range(CC):
                    nc.vector.bn_stats(bn6[:, c, :, :].rearrange("p s m -> p (s m)"),
                                       x_all[:, bass.ds(t.image, 1), c, :].rearrange("p o t -> p (o t)")).then_inc(bn_step, 1)

            def mean_squares(t, n):
                if t is None:
                    return
                dve.wait_ge(bn_step, t.count(BN_OPS, CC + n))
                if n == 0:
                    nc.vector.tensor_tensor(mean_sq[:, :, :], bn6[:, :, :, 1], bn6[:, :, :, 1], ALU.mult).then_inc(bn_step, 1)
                else:
                    nc.vector.scalar_tensor_tensor(out=bn6[:, :, :, 2], in0=bn6[:, :, :, 2], scalar=2.0 / TOKENS, in1=mean_sq[:, :, :],
                                                   op0=ALU.mult, op1=ALU.add).then_inc(bn_step, 1)

            def group_variance(t, n):
                if t is None:
                    return
                if n == 0:
                    dve.wait_ge(group_summed, t.count(1, 1))
                    nc.vector.tensor_copy(g_mom[:, :, :].rearrange("p c m -> p (c m)"), g_cols).then_inc(gn_step, 1)
                else:
                    dve.wait_ge(gn_step, t.count(GN_OPS, n))
                if n == 1:
                    nc.vector.tensor_tensor(g_sq[:, :], g_mom[:, :, 0], g_mom[:, :, 0], ALU.mult).then_inc(gn_step, 1)
                if n == 2:
                    nc.vector.tensor_tensor(g_sq[:, :], g_mom[:, :, 1], g_sq[:, :], ALU.subtract).then_inc(gn_step, 1)
                if n == 3:
                    nc.vector.tensor_scalar(sums[:, NORMS:], g_sq[:, :], 0.0, EPS_GN, ALU.max, ALU.add).then_inc(gn_step, 1)

            def norm_offset(j, base, t):
                if t is None:
                    return
                dve.wait_ge(newton_step, rooted(j, base, 0, 3, 3))
                past(dve, xn32_ready, t.count(2, 0))
                nc.vector.scalar_tensor_tensor(out=g_off[:, :], in0=g_mom[:, :, 0], scalar=-1.0, in1=inv_root[:, NORMS:], op0=ALU.mult, op1=ALU.mult).then_inc(gn_step, 1)

            def normalise(t, c):
                if t is None:
                    return
                dve.wait_ge(gn_step, t.count(GN_OPS, GN_OPS))
                past(dve, xn_ready, t.count(1, 0))
                nc.vector.tensor_scalar(xn32[:, c, :], x_all[:, bass.ds(t.image, 1), c, :].rearrange("p o t -> p (o t)"),
                                        inv_root[:, NORMS + c:NORMS + c + 1], g_off[:, c:c + 1], ALU.mult, ALU.add).then_inc(xn32_ready, 1)

            def sum_norms(t, e):
                if t is None:
                    return
                dve.wait_ge(squared, t.count(2, e + 1))
                nc.vector.tensor_reduce(sums[:, 0:NORMS], squares[:, :].rearrange("p (h d) -> p h d", d=HD), AX_X, ALU.add).then_inc(norms_summed, 1)

            def roots(j, base, e, n):
                at = root_columns(job(j, base, 0), job(j, base, 1) if e == 0 else None)
                if at is None:
                    return
                y, v, tmp = inv_root[:, at], sums[:, at], newton[:, at]
                if n == 0:
                    dve.wait_ge(seeded, rooted(j, base, e, 1))
                    nc.vector.tensor_tensor(tmp, y, y, ALU.mult).then_inc(newton_step, 1)
                else:
                    dve.wait_ge(newton_step, rooted(j, base, e, n, 3))
                if n == 1:
                    nc.vector.scalar_tensor_tensor(out=tmp, in0=tmp, scalar=-0.5, in1=v, op0=ALU.mult, op1=ALU.mult).then_inc(newton_step, 1)
                if n == 2:
                    nc.vector.scalar_tensor_tensor(out=y, in0=tmp, scalar=1.5, in1=y, op0=ALU.add, op1=ALU.mult).then_inc(newton_step, 1)

            def scale_norms(j, base, t, e):
                if t is None:
                    return
                dve.wait_ge(newton_step, rooted(j, base, e, 3, 3))
                nc.vector.scalar_tensor_tensor(out=rnorm[:, :], in0=inv_root[:, 0:NORMS], scalar=INV_NORM_TOP, in1=qk_scale[:, t.layer, :],
                                               op0=ALU.min, op1=ALU.mult).then_inc(rnorm_ready, 1)

            def make_unit(t, e):
                if t is None:
                    return
                dve.wait_ge(rnorm_ready, t.count(2, e + 1))
                past(dve, lo_ready, t.count(4, 2 * e))
                nc.vector.tensor_tensor(unit[:, :].rearrange("p (h d) -> p h d", d=HD), b_qk[e][:, :].rearrange("p (h d) -> p h d", d=HD),
                                        rnorm[:, :].rearrange("p (h o) -> p h o", o=1).broadcast_to([P, NORMS, HD]), ALU.mult).then_inc(unit_ready, 1)

            def keep_k(t, e):
                if t is None:
                    return
                T = t.count(2, e + 1)
                dve.wait_ge(k_turned, T)
                past(dve, scored, t.count(4, 2 * e - 2))
                nc.vector.tensor_copy(k_rows[N:P, e, :, :, N:P].rearrange("p w g m -> p g w m"),
                                      turned[N:P, :, :].rearrange("p g (w m) -> p g w m", w=2)).then_inc(k_ready1, 1)

            def set_shift(t, e):
                if t is None or not t.exact:
                    return
                past(dve, q_refined, t.count_exact(2, e - 1))
                hi, lo = (q_aug[:, t.layer, e, :, 3 * HD + n] for n in range(2))
                nc.vector.tensor_copy(hi, shift32[:, t.layer, :]).then_inc(shift_set, 1)
                dve.wait_ge(shift_set, t.count_exact(4, 2 * e + 1))
                nc.vector.tensor_tensor(lo, shift32[:, t.layer, :], hi, ALU.subtract).then_inc(shift_set, 1)

            def cap(t, e):
                if t is None or not t.exact:
                    return
                for w in range(2):
                    dve.wait_ge(scored, t.count(4, 2 * e + w + 1))
                    nc.vector.tensor_scalar(b_score[w][:, :], b_score[w][:, :], HEADROOM + 1.0, None, ALU.min).then_inc(capped, 1)

            def refine_shift(t, e):
                if t is None or not t.exact:
                    return
                step = lambda n: t.count_exact(16, 8 * e + n)
                dve.wait_ge(q_scored, t.count_exact(2, e + 1))
                half = PAIRS
                for b in range(2):
                    if b:
                        dve.wait_ge(shift_step, step(2))
                    nc.vector.tensor_tensor(allowed[:, :, :], b_score[b][:, :].rearrange("p (h m) -> p h m", m=N),
                                            hide[:, e, :].rearrange("p (o m) -> p o m", o=1).broadcast_to([P, half, N]), ALU.add).then_inc(shift_step, 1)
                    dve.wait_ge(shift_step, step(2 * b + 1))
                    nc.vector.tensor_reduce(row_max[:, half * b:half * (b + 1)], allowed[:, :, :], AX_X, ALU.max).then_inc(shift_step, 1)
                dve.wait_ge(shift_step, step(4))
                nc.vector.tensor_scalar(row_shift[:, :], row_max[:, :], -1.0, HEADROOM, ALU.mult, ALU.add).then_inc(shift_step, 1)
                dve.wait_ge(shift_step, step(5))
                nc.vector.tensor_tensor(row_shift[:, :], row_shift[:, :], shift32[:, t.layer, :], ALU.add).then_inc(shift_step, 1)
                dve.wait_ge(shift_step, step(6))
                dve.wait_ge(q_turned, t.count(2, e + 1))
                hi, lo = (q_aug[:, t.layer, e, :, 3 * HD + n] for n in range(2))
                nc.vector.tensor_copy(hi, row_shift[:, :]).then_inc(shift_step, 1)
                dve.wait_ge(shift_step, step(7))
                nc.vector.tensor_tensor(lo, row_shift[:, :], hi, ALU.subtract).then_inc(shift_step, 1)

            def invert_sums(t, e):
                if t is None:
                    return
                dve.wait_ge(mix_done, t.count(2, e + 1))
                past(dve, sums_spread, t.count(8, 4 * e))
                nc.vector.reciprocal(inv_sums[:, :], sum_rows[e]).then_inc(sums_inverted, 1)

            def spread_sums(t, e):
                if t is None:
                    return
                dve.wait_ge(sums_inverted, t.count(2, e + 1))
                past(dve, mixed_ready, t.count(2, e))
                past(dve, sums_seen, t.count(2, e))
                nc.vector.tensor_tensor(top_inverse[:, :], top_inverse[:, :], inv_sums[:, :], ALU.max).then_inc(sums_seen, 1)
                for w in range(2):
                    for c in range(CC):
                        nc.vector.stream_shuffle(r_sum[:, c, w * N:(w + 1) * N], inv_sums[:, :],
                                                 [4 * w + 2 * c + p // HD for p in range(32)]).then_inc(sums_spread, 1)

            def divide(t, e):
                if t is None:
                    return
                dve.wait_ge(sums_spread, t.count(8, 4 * e + 4))
                past(dve, z_done, t.count(2, e - 1))
                nc.vector.scalar_tensor_tensor(out=mixed[:, e, :, :], in0=r_sum[:, :, :], scalar=INVERSE_CAP, in1=mix_cols[e],
                                               op0=ALU.min, op1=ALU.mult).then_inc(mixed_ready, 1)

            def add_residual(t, e, c):
                if t is None:
                    return
                if c == 0:
                    dve.wait_ge(z_done, t.count(2, e + 1))
                    if t.layer and e == 0:
                        past(dve, out_stored[t.parity], t.stores(16))
                at = slice(e * P, (e + 1) * P)
                here = x_all[:, bass.ds(t.image, 1), c, at].rearrange("p o t -> p (o t)")
                ins = nc.vector.scalar_tensor_tensor(out=x_out[:, t.parity, c, at] if t.layer else here, in0=z_cols[:, c, :],
                                                     scalar=out_bias[:, t.layer, c:c + 1], in1=here, op0=ALU.add, op1=ALU.add)
                if c == CC - 1:
                    ins.then_inc(x_updated, 1)

            def repeat_hi(t, e, n):
                if t is None:
                    return
                dve.wait_ge(hi_ready, t.count(4, 2 * e + n + 1))
                rows, at = ((q_aug[:, t.layer, e, :, :], HD), (k_aug[:, e, :, :], 2 * HD))[n]
                nc.vector.tensor_copy(rows[:, :, at:at + HD], rows[:, :, 0:HD]).then_inc(hi_again, 1)

            def iteration(j, base):
                after = job(j, base, 1)
                if j in (1, 4) and not base.exact:
                    mask_bias((1, 4).index(j))
                for e in range(2):
                    now, done = tile(j, base, e, 0), tile(j, base, e, 5)
                    g, late_g, moments_of = (after, None, None) if e == 0 else (None, after, job(j, base, 2))
                    invert_sums(*done)
                    normalise(late_g, 0)
                    spread_sums(*done)
                    normalise(late_g, 1)
                    divide(*done)
                    group_moments(moments_of)
                    group_variance(g, 0)
                    group_variance(g, 1)
                    mean_squares(moments_of, 0)
                    sum_norms(*now)
                    group_variance(g, 2)
                    group_variance(g, 3)
                    keep_k(*tile(j, base, e, 2))
                    roots(j, base, e, 0)
                    add_residual(*done, 0)
                    roots(j, base, e, 1)
                    add_residual(*done, 1)
                    roots(j, base, e, 2)
                    repeat_hi(*tile(j, base, e, 1), 0)
                    norm_offset(j, base, g)
                    mean_squares(moments_of, 1)
                    scale_norms(j, base, *now)
                    repeat_hi(*tile(j, base, e, 1), 1)
                    make_unit(*now)
                    set_shift(*tile(j, base, e, 1))
                    cap(*tile(j, base, e, 3))
                    refine_shift(*tile(j, base, e, 2))

            def raise_flag():
                dve.wait_ge(sums_seen, 2 * JOBS)
                nc.vector.tensor_reduce(lost[:, :], top_inverse[:, :], AX_X, ALU.max).then_inc(flag_step, 1)
                dve.wait_ge(flag_step, 1)
                dve.wait_ge(x_updated, 2 * JOBS)
                nc.vector.tensor_scalar(lost[:, :], lost[:, :], INVERSE_TOP, None, ALU.is_gt).then_inc(flag_step, 1)
                dve.wait_ge(flag_summed, 1)
                nc.vector.tensor_copy(flag[:, :], ps[3][0:1, 0:1]).then_inc(flag_ready, 1)

            both_passes(dve, iteration, raise_flag)

        @block.gpsimd
        def _(pool):
            nc.gpsimd.memset(q_aug[:, :, :, :, :], 0.0).then_inc(su_pool, 1)
            nc.gpsimd.memset(top_inverse[:, :], 0.0).then_inc(su_pool, 1)
            nc.gpsimd.memset(k_aug[:, :, :, :], 0.0).then_inc(aug_zero, 1)
            nc.gpsimd.memset(k_rows[:, :, :, :, :], 0.0).then_inc(aug_zero, 1)
            nc.gpsimd.memset(v_pair[:, :, :, :, :], 0.0).then_inc(aug_zero, 1)
            pool.wait_ge(aug_zero, 3)
            pool.wait_ge(su_pool, 1)
            nc.gpsimd.memset(k_aug[:, :, :, 3 * HD:3 * HD + 2], 1.0).then_inc(aug_zero, 1)
            pool.wait_ge(aug_zero, 4)

            def split_xn(t):
                if t is None:
                    return
                pool.wait_ge(xn_hi, t.count(1, 1))
                past(pool, v_done, t.count(2, -2))
                nc.gpsimd.tensor_tensor(xn[:, 1, t.parity, :, :], xn32[:, :, :], xn[:, 0, t.parity, :, :], ALU.subtract).then_inc(xn_ready, 1)

            def split_lo(t, e):
                if t is None:
                    return
                pool.wait_ge(hi_ready, t.count(4, 2 * e + 2))
                for n, dst, hi in ((0, q_aug[:, t.layer, e, :, 2 * HD:3 * HD], q_aug[:, t.layer, e, :, 0:HD]),
                                   (1, k_aug[:, e, :, HD:2 * HD], k_aug[:, e, :, 0:HD])):
                    nc.gpsimd.tensor_tensor(dst, unit[:, n * D:(n + 1) * D].rearrange("p (h d) -> p h d", d=HD), hi, ALU.subtract).then_inc(lo_ready, 1)

            def weigh(t, e):
                if t is None:
                    return
                for w in range(2):
                    pool.wait_ge(exped, t.count(4, 2 * e + w + 1))
                    pr = probs[:, 2 * e + w, :, :]
                    nc.gpsimd.tensor_tensor(pr, pr, exp_bias[:, t.layer, 2 * e + w, :, :], ALU.mult).then_inc(weighted, 1)


            def iteration(j, base):
                if j in (1, 5) and not base.exact:
                    pool.wait_ge(bias_ready, 4 * ((1, 5).index(j) + 1))
                for e in range(2):
                    split_lo(*tile(j, base, e, 1))
                    if e == 1:
                        split_xn(job(j, base, 1))
                    weigh(*tile(j, base, e, 3))

            both_passes(pool, iteration)


_WEIGHTS = ['Wq', 'Wk', 'Wv', 'bv', 'Wo', 'bo', 'logit_scale', 'cpb_w1', 'cpb_b1', 'cpb_w2']


def _constants():
    import numpy as np
    group = D // 32
    r = np.arange(-(WIN - 1), WIN, dtype=np.float32)
    t = np.stack(np.meshgrid(r, r, indexing="ij"), axis=-1) / (WIN - 1) * 8.0
    t = np.sign(t) * np.log2(np.abs(t) + 1.0) / 3.0
    t = t.reshape(-1, 2)[::-1].T
    pos = np.arange(N)
    low_r, low_c = pos // WIN < WIN - SHIFT, pos % WIN < WIN - SHIFT
    same = [np.ones((N, N), bool), low_c[:, None] == low_c[None, :], low_r[:, None] == low_r[None, :]]
    same.append(same[1] & same[2])
    own = {
        "group_mean": np.kron(np.eye(P // group), np.full((group, group), 0.5 / group)),
        "sum_cols": np.stack([np.kron(np.eye(2), np.ones((N, 1))) @ np.tile(np.eye(8)[2 * i:2 * i + 2], 4) for i in range(4)], 1),
        "act_bias": np.tile([-BIAS_MID, LN_SCALE * LN_FLOOR, 0.5 * math.log(LN_SCALE), 1.0], (P, 1)),
        "hide": np.stack([np.where(np.concatenate(same[2 * e:2 * e + 2]), 0.0, HIDDEN) for e in range(2)], 1),
        "masks": np.tile(np.stack(same, 1), (2, 1, 1)),
    }
    return {
        "ident16": np.eye(P, dtype=np.float16),
        "coords": np.concatenate([t, np.ones((1, REL * REL))]).astype(np.float32),
        "consts32": np.concatenate([own[n].reshape(P, cols) for n, cols in CONST_COLS.items()], axis=1).astype(np.float32),
    }


def _to_channels(x):
    import numpy as np
    x = np.roll(x, (-SHIFT, -SHIFT), axis=(1, 2))
    x = x.reshape(IMAGES, SIDE // WIN, WIN, SIDE // WIN, WIN, CC, P)
    return x.transpose(6, 0, 5, 1, 3, 2, 4).reshape(P, IMAGES, CC, TOKENS)


def _from_channels(y):
    import numpy as np
    y = y.reshape(P, IMAGES, CC, SIDE // WIN, SIDE // WIN, WIN, WIN)
    y = y.transpose(1, 3, 5, 4, 6, 2, 0).reshape(IMAGES, SIDE, SIDE, D)
    return np.roll(y, (SHIFT, SHIFT), axis=(1, 2))


def kernel(**inputs):
    import numpy as _np
    import concourse.bacc as _bacc
    from concourse import mybir as _mybir
    from concourse.bass_utils import run_bass_kernel_spmd as _run

    nc = _bacc.Bacc("TRN2", target_bir_lowering=False, num_devices=1)
    arrays = {}

    def put(name, a):
        a = _np.ascontiguousarray(a)
        arrays[name] = a
        return nc.dram_tensor(name, a.shape, _mybir.dt.from_np(a.dtype), kind="ExternalInput").ap()

    x = put("in_x", _to_channels(_np.asarray(inputs["x"])))
    weights = []
    for l in range(LAYERS):
        w = {n: _np.asarray(inputs[f"L{l}_conv_{n}"]) for n in _WEIGHTS}
        laid = {
            "matrices": _np.concatenate([w[n].T for n in ("Wq", "Wk", "Wv", "Wo")], axis=1),
            "biases": _np.stack([w[n].reshape(CC, P).T for n in ("bv", "bo")], axis=1),
            "cpb1": _np.concatenate([w["cpb_w1"].T, w["cpb_b1"][None]]),
            "cpb2": w["cpb_w2"].T,
            "logit_scale": w["logit_scale"].reshape(HEADS),
        }
        weights.append({n: put(f"in_L{l}_{n}", a) for n, a in laid.items()})
    consts = {name: put(f"const_{name}", a) for name, a in _constants().items()}
    scratch = nc.dram_tensor("table_scratch", (LAYERS, HEADS, REL * REL), F32, kind="Internal").ap()
    out = nc.dram_tensor("out_0", (P, IMAGES, CC, TOKENS), F32, kind="ExternalOutput").ap()
    build(nc, x, weights, out, consts, scratch)
    r = _run(nc, [arrays], core_ids=[0])
    return _from_channels(r.results[0]["out_0"])
```
